# Optimizing a Trainium2 kernel written in Bass

```python
import numpy as np
import jax
import jax.numpy as jnp

def _softmax(x, axis=-1):
    return jax.nn.softmax(x, axis=axis)

def _gelu(x):
    return jax.nn.gelu(x, approximate=True)

def _silu(x):
    return jax.nn.silu(x)

def _sigmoid(x):
    return jax.nn.sigmoid(x)

def _layernorm(x, axis=-1, eps=1e-05):
    m = jnp.mean(x, axis=axis, keepdims=True)
    v = jnp.var(x, axis=axis, keepdims=True)
    return (x - m) / jnp.sqrt(v + eps)

def _scatter_add(tgt, idx, src, axis=0):
    return tgt.at[idx].add(src)

def _segment_sum(src, seg, n):
    return jax.ops.segment_sum(src, seg, n)
kernel_name = 'mk_cond_seq_d2_seqx_r4_c72371'

def setup_inputs(seed: int=0):
    np.random.seed(seed)
    _w = jnp.asarray

    def _rec_inputs():
        import jax
        import jax.numpy as jnp
        _rk = jax.random.key(seed)
        x = -0.0002928 + 1 * jax.random.normal(jax.random.fold_in(_rk, 1), (8, 256, 256), jnp.float32)
        _lenS = 256 - jax.random.randint(jax.random.fold_in(_rk, 7), (8,), 0, max(1, 256 // 4) + 1, jnp.int32)
        _lenS2 = 256 - jax.random.randint(jax.random.fold_in(_rk, 8), (8,), 0, max(1, 256 // 4) + 1, jnp.int32)
        cond_2048 = 0.0061147 + 1.02565 * jax.random.normal(jax.random.fold_in(_rk, 11), (8, 512), jnp.float32)
        _validS = jnp.arange(256)[None, :] < _lenS[:, None]
        _validS2 = jnp.arange(256)[None, :] < _lenS2[:, None]
        _causal = jnp.tril(jnp.ones((256, 256), dtype=bool))
        mask_BxSx1_fk1 = jnp.where(jnp.ones((8, 256, 1), dtype=bool), 1.0, 0.0).astype(jnp.float32)
        return (x, cond_2048, mask_BxSx1_fk1)
    x, cond_2048, mask_BxSx1_fk1 = _rec_inputs()

    def _L0_cond_setup():
        import jax, jax.numpy as jnp
        import numpy as np
        D = 256
        DI = 512
        N = 16
        DT_RANK = 64
        D_CONV = 4
        EPS = 1e-05

        def _layernorm(x, g, b):
            mu = jnp.mean(x, axis=-1, keepdims=True)
            var = jnp.mean((x - mu) ** 2, axis=-1, keepdims=True)
            return (x - mu) * jax.lax.rsqrt(var + EPS) * g + b

        def _mamba(xn, in_proj_w, conv_w, conv_b, x_proj_w, dt_proj_w, dt_proj_b, A_log, D_param, out_proj_w):
            b, sl, _ = xn.shape
            xz = jnp.einsum('bsd,ed->bse', xn, in_proj_w)
            x_in, z = jnp.split(xz, 2, axis=-1)
            xt = jnp.transpose(x_in, (0, 2, 1))
            u = jax.lax.conv_general_dilated(xt, conv_w[:, None, :], (1,), [(D_CONV - 1, 0)], feature_group_count=DI, dimension_numbers=('NCH', 'OIH', 'NCH')) + conv_b[None, :, None]
            u = jax.nn.silu(jnp.transpose(u, (0, 2, 1)))
            x_dbl = jnp.einsum('bsd,ed->bse', u, x_proj_w)
            dt_r, B, C = jnp.split(x_dbl, [DT_RANK, DT_RANK + N], axis=-1)
            dt = jax.nn.softplus(jnp.einsum('bsr,dr->bsd', dt_r, dt_proj_w) + dt_proj_b)
            A = -jnp.exp(A_log)

            def step(h, inp):
                dt_t, B_t, C_t, u_t = inp
                dA = jnp.exp(dt_t[:, :, None] * A)
                h = h * dA + (dt_t * u_t)[:, :, None] * B_t[:, None, :]
                y = jnp.einsum('bdn,bn->bd', h, C_t)
                return (h, y)
            seq = (jnp.transpose(dt, (1, 0, 2)), jnp.transpose(B, (1, 0, 2)), jnp.transpose(C, (1, 0, 2)), jnp.transpose(u, (1, 0, 2)))
            h0 = jnp.zeros((b, DI, N), xn.dtype)
            _, ys = jax.lax.scan(step, h0, seq)
            y = jnp.transpose(ys, (1, 0, 2)) + u * D_param
            y = y * jax.nn.silu(z)
            return jnp.einsum('bsd,ed->bse', y, out_proj_w)
        key = jax.random.key(seed)
        ks = jax.random.split(key, 16)
        s = lambda fan: 1.0 / np.sqrt(fan)
        inp = {'x': jax.random.normal(ks[0], (2, 512, D), jnp.float32), 'c': jax.random.normal(ks[1], (2, 2 * D), jnp.float32), 'ln_g': jnp.ones((D,), jnp.float32), 'ln_b': jnp.zeros((D,), jnp.float32), 'ada_w': jax.random.normal(ks[2], (3 * D, 2 * D), jnp.float32) * s(2 * D), 'ada_b': jnp.zeros((3 * D,), jnp.float32), 'in_proj_w': jax.random.normal(ks[3], (2 * DI, D), jnp.float32) * s(D), 'conv_w': jax.random.normal(ks[4], (DI, D_CONV), jnp.float32) * s(D_CONV), 'conv_b': jnp.zeros((DI,), jnp.float32), 'x_proj_w': jax.random.normal(ks[5], (DT_RANK + 2 * N, DI), jnp.float32) * s(DI), 'dt_proj_w': jax.random.normal(ks[6], (DI, DT_RANK), jnp.float32) * s(DT_RANK), 'dt_proj_b': jax.random.uniform(ks[7], (DI,), jnp.float32, -4.0, -2.0), 'A_log': jnp.tile(jnp.log(jnp.arange(1, N + 1, dtype=jnp.float32)), (DI, 1)), 'D_param': jnp.ones((DI,), jnp.float32), 'out_proj_w': jax.random.normal(ks[8], (D, DI), jnp.float32) * s(DI)}
        return inp
    _L0_cond_all = _L0_cond_setup()
    _L0_cond_in = {k: v for k, v in _L0_cond_all.items() if k in ('ln_g', 'ln_b', 'ada_w', 'ada_b', 'in_proj_w', 'conv_w', 'conv_b', 'x_proj_w', 'dt_proj_w', 'dt_proj_b', 'A_log', 'D_param', 'out_proj_w')}
    del _L0_cond_all

    def _L1_cond_setup():
        import jax, jax.numpy as jnp
        import numpy as np
        B, T, D, H, TE = (4, 512, 256, 8, 512)
        EPS = 1e-05

        def _ln(x, w, b):
            m = jnp.mean(x, axis=-1, keepdims=True)
            v = jnp.mean((x - m) ** 2, axis=-1, keepdims=True)
            return (x - m) * jax.lax.rsqrt(v + EPS) * w + b
        key = jax.random.key(seed)
        ks = jax.random.split(key, 16)
        s = 0.02
        inp = {'x': jax.random.normal(ks[0], (B, T, D), jnp.float32), 'emb': jax.random.normal(ks[1], (B, TE), jnp.float32), 'src_mask': (jax.random.uniform(ks[2], (B, T, 1)) > 0.2).astype(jnp.float32), 'num_head': H, 'ln_w': jnp.ones((D,), jnp.float32), 'ln_b': jnp.zeros((D,), jnp.float32), 'Wq': jax.random.normal(ks[3], (D, D), jnp.float32) * s, 'bq': jnp.zeros((D,), jnp.float32), 'Wk': jax.random.normal(ks[4], (D, D), jnp.float32) * s, 'bk': jnp.zeros((D,), jnp.float32), 'Wv': jax.random.normal(ks[5], (D, D), jnp.float32) * s, 'bv': jnp.zeros((D,), jnp.float32), 'W_emb': jax.random.normal(ks[6], (TE, 2 * D), jnp.float32) * s, 'b_emb': jnp.zeros((2 * D,), jnp.float32), 'ln2_w': jnp.ones((D,), jnp.float32), 'ln2_b': jnp.zeros((D,), jnp.float32), 'W_out': jax.random.normal(ks[7], (D, D), jnp.float32) * s, 'b_out': jnp.zeros((D,), jnp.float32)}
        return inp
    _L1_cond_all = _L1_cond_setup()
    _L1_cond_in = {k: v for k, v in _L1_cond_all.items() if k in ('ln_w', 'ln_b', 'Wq', 'bq', 'Wk', 'bk', 'Wv', 'bv', 'W_emb', 'b_emb', 'ln2_w', 'ln2_b', 'W_out', 'b_out')}
    del _L1_cond_all
    return {'x': x, 'cond_2048': cond_2048, 'mask_BxSx1_fk1': mask_BxSx1_fk1, 'L0_cond_ln_g': _L0_cond_in['ln_g'], 'L0_cond_ln_b': _L0_cond_in['ln_b'], 'L0_cond_ada_w': _L0_cond_in['ada_w'], 'L0_cond_ada_b': _L0_cond_in['ada_b'], 'L0_cond_in_proj_w': _L0_cond_in['in_proj_w'], 'L0_cond_conv_w': _L0_cond_in['conv_w'], 'L0_cond_conv_b': _L0_cond_in['conv_b'], 'L0_cond_x_proj_w': _L0_cond_in['x_proj_w'], 'L0_cond_dt_proj_w': _L0_cond_in['dt_proj_w'], 'L0_cond_dt_proj_b': _L0_cond_in['dt_proj_b'], 'L0_cond_A_log': _L0_cond_in['A_log'], 'L0_cond_D_param': _L0_cond_in['D_param'], 'L0_cond_out_proj_w': _L0_cond_in['out_proj_w'], 'L1_cond_ln_w': _L1_cond_in['ln_w'], 'L1_cond_ln_b': _L1_cond_in['ln_b'], 'L1_cond_Wq': _L1_cond_in['Wq'], 'L1_cond_bq': _L1_cond_in['bq'], 'L1_cond_Wk': _L1_cond_in['Wk'], 'L1_cond_bk': _L1_cond_in['bk'], 'L1_cond_Wv': _L1_cond_in['Wv'], 'L1_cond_bv': _L1_cond_in['bv'], 'L1_cond_W_emb': _L1_cond_in['W_emb'], 'L1_cond_b_emb': _L1_cond_in['b_emb'], 'L1_cond_ln2_w': _L1_cond_in['ln2_w'], 'L1_cond_ln2_b': _L1_cond_in['ln2_b'], 'L1_cond_W_out': _L1_cond_in['W_out'], 'L1_cond_b_out': _L1_cond_in['b_out']}

def reference(x, cond_2048, mask_BxSx1_fk1, L0_cond_ln_g, L0_cond_ln_b, L0_cond_ada_w, L0_cond_ada_b, L0_cond_in_proj_w, L0_cond_conv_w, L0_cond_conv_b, L0_cond_x_proj_w, L0_cond_dt_proj_w, L0_cond_dt_proj_b, L0_cond_A_log, L0_cond_D_param, L0_cond_out_proj_w, L1_cond_ln_w, L1_cond_ln_b, L1_cond_Wq, L1_cond_bq, L1_cond_Wk, L1_cond_bk, L1_cond_Wv, L1_cond_bv, L1_cond_W_emb, L1_cond_b_emb, L1_cond_ln2_w, L1_cond_ln2_b, L1_cond_W_out, L1_cond_b_out):
    import jax
    import jax.numpy as jnp

    def _L0_cond_ref(x, c, ln_g, ln_b, ada_w, ada_b, in_proj_w, conv_w, conv_b, x_proj_w, dt_proj_w, dt_proj_b, A_log, D_param, out_proj_w):
        import jax, jax.numpy as jnp
        import numpy as np
        D = 256
        DI = 512
        N = 16
        DT_RANK = 64
        D_CONV = 4
        EPS = 1e-05

        def _layernorm(x, g, b):
            mu = jnp.mean(x, axis=-1, keepdims=True)
            var = jnp.mean((x - mu) ** 2, axis=-1, keepdims=True)
            return (x - mu) * jax.lax.rsqrt(var + EPS) * g + b

        def _mamba(xn, in_proj_w, conv_w, conv_b, x_proj_w, dt_proj_w, dt_proj_b, A_log, D_param, out_proj_w):
            b, sl, _ = xn.shape
            xz = jnp.einsum('bsd,ed->bse', xn, in_proj_w)
            x_in, z = jnp.split(xz, 2, axis=-1)
            xt = jnp.transpose(x_in, (0, 2, 1))
            u = jax.lax.conv_general_dilated(xt, conv_w[:, None, :], (1,), [(D_CONV - 1, 0)], feature_group_count=DI, dimension_numbers=('NCH', 'OIH', 'NCH')) + conv_b[None, :, None]
            u = jax.nn.silu(jnp.transpose(u, (0, 2, 1)))
            x_dbl = jnp.einsum('bsd,ed->bse', u, x_proj_w)
            dt_r, B, C = jnp.split(x_dbl, [DT_RANK, DT_RANK + N], axis=-1)
            dt = jax.nn.softplus(jnp.einsum('bsr,dr->bsd', dt_r, dt_proj_w) + dt_proj_b)
            A = -jnp.exp(A_log)

            def step(h, inp):
                dt_t, B_t, C_t, u_t = inp
                dA = jnp.exp(dt_t[:, :, None] * A)
                h = h * dA + (dt_t * u_t)[:, :, None] * B_t[:, None, :]
                y = jnp.einsum('bdn,bn->bd', h, C_t)
                return (h, y)
            seq = (jnp.transpose(dt, (1, 0, 2)), jnp.transpose(B, (1, 0, 2)), jnp.transpose(C, (1, 0, 2)), jnp.transpose(u, (1, 0, 2)))
            h0 = jnp.zeros((b, DI, N), xn.dtype)
            _, ys = jax.lax.scan(step, h0, seq)
            y = jnp.transpose(ys, (1, 0, 2)) + u * D_param
            y = y * jax.nn.silu(z)
            return jnp.einsum('bsd,ed->bse', y, out_proj_w)
        ada = jnp.einsum('bc,ec->be', jax.nn.silu(c), ada_w) + ada_b
        shift, scale, gate = jnp.split(ada, 3, axis=1)
        xn = _layernorm(x, ln_g, ln_b)
        xn = xn * (1.0 + scale[:, None, :]) + shift[:, None, :]
        x_ssm = _mamba(xn, in_proj_w, conv_w, conv_b, x_proj_w, dt_proj_w, dt_proj_b, A_log, D_param, out_proj_w)
        return x + gate[:, None, :] * x_ssm

    def _L1_cond_ref(x, emb, src_mask, num_head, ln_w, ln_b, Wq, bq, Wk, bk, Wv, bv, W_emb, b_emb, ln2_w, ln2_b, W_out, b_out):
        import jax, jax.numpy as jnp
        import numpy as np
        B, T, D, H, TE = (4, 512, 256, 8, 512)
        EPS = 1e-05

        def _ln(x, w, b):
            m = jnp.mean(x, axis=-1, keepdims=True)
            v = jnp.mean((x - m) ** 2, axis=-1, keepdims=True)
            return (x - m) * jax.lax.rsqrt(v + EPS) * w + b
        b, t, d = x.shape
        h = num_head
        dh = d // h
        xn = _ln(x, ln_w, ln_b)
        q = xn @ Wq + bq
        k = xn @ Wk + bk + (1.0 - src_mask) * -1000000.0
        q = jax.nn.softmax(q.reshape(b, t, h, dh), axis=-1)
        k = jax.nn.softmax(k.reshape(b, t, h, dh), axis=1)
        v = ((xn @ Wv + bv) * src_mask).reshape(b, t, h, dh)
        att = jnp.einsum('bnhd,bnhl->bhdl', k, v)
        y = jnp.einsum('bnhd,bhdl->bnhl', q, att).reshape(b, t, d)
        emb_out = (jax.nn.silu(emb) @ W_emb + b_emb)[:, None, :]
        scale, shift = jnp.split(emb_out, 2, axis=2)
        hh = _ln(y, ln2_w, ln2_b) * (1.0 + scale) + shift
        hh = jax.nn.silu(hh) @ W_out + b_out
        return x + hh
    x = _L0_cond_ref(x, cond_2048, L0_cond_ln_g, L0_cond_ln_b, L0_cond_ada_w, L0_cond_ada_b, L0_cond_in_proj_w, L0_cond_conv_w, L0_cond_conv_b, L0_cond_x_proj_w, L0_cond_dt_proj_w, L0_cond_dt_proj_b, L0_cond_A_log, L0_cond_D_param, L0_cond_out_proj_w)
    x = _L1_cond_ref(x, cond_2048, mask_BxSx1_fk1, 8, L1_cond_ln_w, L1_cond_ln_b, L1_cond_Wq, L1_cond_bq, L1_cond_Wk, L1_cond_bk, L1_cond_Wv, L1_cond_bv, L1_cond_W_emb, L1_cond_b_emb, L1_cond_ln2_w, L1_cond_ln2_b, L1_cond_W_out, L1_cond_b_out)
    return x

_drawn_inputs = setup_inputs


def setup_inputs(seed=0):
    import zlib

    import numpy as np

    out = dict(_drawn_inputs(seed))
    spreads = {'L0_cond_ln_g': (1.0, 0.2),
     'L0_cond_ln_b': (0.0, 0.1),
     'L0_cond_ada_b': (0.0, 0.1),
     'L0_cond_conv_b': (0.0, 0.1),
     'L0_cond_D_param': (1.0, 0.2),
     'L1_cond_ln_w': (1.0, 0.6),
     'L1_cond_ln_b': (0.0, 0.1),
     'L1_cond_bq': (0.0, 0.8),
     'L1_cond_bk': (0.0, 0.8),
     'L1_cond_bv': (0.0, 0.1),
     'L1_cond_b_emb': (0.0, 0.348),
     'L1_cond_ln2_w': (1.0, 0.2),
     'L1_cond_ln2_b': (0.0, 0.384),
     'L1_cond_b_out': (0.0, 0.1)}
    factors = {'L1_cond_Wq': 8.0, 'L1_cond_Wk': 8.0}
    for name, (base, spread) in spreads.items():
        noise = np.random.default_rng([zlib.crc32(name.encode()), seed]).standard_normal(out[name].shape)
        drawn = base * np.exp(spread * noise) if base else spread * noise
        out[name] = jnp.asarray(drawn.astype(out[name].dtype))
    for name, factor in factors.items():
        out[name] = (out[name] * factor).astype(out[name].dtype)
    return out
```

```python
from contextlib import ExitStack

import concourse.bass as bass
from concourse import mybir

F32 = mybir.dt.float32
ALU = mybir.AluOpType
ACT = mybir.ActivationFunctionType
AX = mybir.AxisListType

P = 128
NB, T, D, DI, N = 8, 256, 256, 512, 16
RANK, TAPS, HEADS = 64, 4, 8
DH = D // HEADS
KC = 512 // P
KD = D // P
DC = DI // P
TC = T // P
NQ = 4
UPC = N // NQ
U = DC * UPC
NU = NQ * T
EPS = 1e-5
BIG = 1e37
MASKED = 1e6
DBUF, HBUF, XBUF = 3, 2, 3

COLS = {}
_at = 0
for _name, _n in (("A_log", DC * N), ("conv_w", DC * TAPS), ("conv_b", DC), ("dt_b", DC), ("D_par", DC), ("ln_g", KD),
                  ("ln_b", KD), ("ada_b", 2 * KD), ("emb_b", 2 * KD), ("ln1_w", KD), ("ln1_b", KD), ("ln2_w", KD),
                  ("ln2_b", KD), ("mask", NB * TC)):
    COLS[_name] = (_at, _at + _n)
    _at += _n
NPAR = _at


def build(nc, a, out):
    ctx = ExitStack()
    with ctx:
        def sb(name, shape):
            return ctx.enter_context(nc.sbuf_tensor(name, shape, F32))

        def ps(name, shape):
            return ctx.enter_context(nc.psum_tensor(name, shape, F32))

        def sem(name):
            return ctx.enter_context(nc.semaphore(name))

        par = sb("par", [P, NPAR])
        ident = sb("ident", [P, P])
        blockmask = sb("blockmask", [P, P])
        cT = sb("cT", [P, KC, NB])
        win = sb("win", [P, KD, 2 * DI])
        wxp = sb("wxp", [P, DC, RANK + 2 * N])
        wdt = sb("wdt", [RANK, DI])
        wo = sb("wo", [P, DC, D])
        wqkvo = sb("wqkvo", [P, 4, KD, D])
        klhs = sb("klhs", [33, D])
        krhs = sb("krhs", [33, NB * T])
        brow = sb("brow", [1, 3, D])
        gb8 = sb("gb8", [NB, D])
        gate8 = sb("gate8", [NB, D])
        gate = sb("gate", [P, NB, D])
        mods = sb("mods", [P, 4 * KD, NB])
        m0s, m0b = sb("m0s", [P, KD, NB]), sb("m0b", [P, KD, NB])
        m1s, m1b = sb("m1s", [P, KD, NB]), sb("m1b", [P, KD, NB])
        Aneg = sb("Aneg", [P, DC * N])
        mhalf = sb("mhalf", [P, TC])
        xg = sb("xg", [P, XBUF, TC, D])
        st0, mv0 = sb("st0", [P, TC, 6]), sb("mv0", [P, TC, 2])
        ve0, rs0 = sb("ve0", [P, TC]), sb("rs0", [P, TC])
        xhat = sb("xhat", [P, TC, D])
        xnT = sb("xnT", [P, KD, T])
        u = sb("u", [P, 2, DC, T])
        zs = sb("zs", [P, 2, DC, T])
        xdbl = sb("xdbl", [RANK + 2 * N, T])
        conv = sb("conv", [P, DC, T])
        vln = conv
        dt, dtu = sb("dt", [P, 2, DC, T]), sb("dtu", [P, 2, DC, T])
        BC = sb("BC", [P, 2, 2 * N, T])
        dBu = sb("dBu", [P, DBUF, NQ, T])
        hC = sb("hC", [P, HBUF, NQ, T])
        yg = sb("yg", [P, DC, T])
        x1 = sb("x1", [P, TC, D])
        st1, mv1 = sb("st1", [P, TC, 6]), sb("mv1", [P, TC, 2])
        ve1, rs1 = sb("ve1", [P, TC]), sb("rs1", [P, TC])
        xh = sb("xh", [P, TC, D])
        xT = sb("xT", [P, KD, T])
        qmax, qsum, rq = sb("qmax", [P, TC, HEADS]), sb("qsum", [P, TC, HEADS]), sb("rq", [P, TC, HEADS])
        qe = sb("qe", [P, TC, D])
        kmax, ksum, rk = sb("kmax", [P, KD]), sb("ksum", [P, KD]), sb("rk", [P, KD])
        ke = sb("ke", [P, KD, T])
        vm = sb("vm", [P, TC, D])
        qT, kT = sb("qT", [P, KD, T]), sb("kT", [P, TC, D])
        att = sb("att", [P, KD, P])
        yq = qe
        st2, mv2 = sb("st2", [P, TC, 6]), sb("mv2", [P, TC, 2])
        ve2, rs2 = sb("ve2", [P, TC]), sb("rs2", [P, TC])
        fin = sb("fin", [P, TC, D])
        bc_dram = nc.dram_tensor("bc_rows", (2, 2 * N, T), F32, kind="Internal").ap()

        ring = ps("ring", [P, 2, NQ, T])
        YB = ps("YB", [P, T])
        PX = ps("PX", [P, 2, T])
        PY = ps("PY", [P, 2, T])
        PZ = ps("PZ", [P, 2, T])

        adaT = BC[:, 1, 0:3 * KC, :].rearrange("p (k s) e -> p k s e", k=KC)
        embT = BC[:, 1, 3 * KC:5 * KC, :].rearrange("p (k s) e -> p k s e", k=KC)

        s_ld_par = sem("ld_par")
        s_ld_ada = sem("ld_ada")
        s_ld_win = sem("ld_win")
        s_ld_small = sem("ld_small")
        s_ld_w = sem("ld_w")
        s_ld_post = sem("ld_post")
        s_pool_const = sem("pool_const")
        s_sc_ready = sem("sc_ready")
        s_aexp_ready = sem("aexp_ready")
        s_aneg_ready = sem("aneg_ready")
        s_mod_mm = sem("mod_mm")
        s_mod_ready = sem("mod_ready")
        s_m0_ready = sem("m0_ready")
        s_gate8_ready = sem("gate8_ready")
        s_gate_mm = sem("gate_mm")
        s_gate_ready = sem("gate_ready")
        s_krow_ready = sem("krow_ready")
        s_st0_ready = sem("st0_ready")
        s_ve0_ready = sem("ve0_ready")
        s_rs0_ready = sem("rs0_ready")
        s_xhat_ready = sem("xhat_ready")
        s_xT_mm = sem("xT_mm")
        s_xn_ready = sem("xn_ready")
        s_xz_mm = sem("xz_mm")
        s_conv0_ready = sem("conv0_ready")
        s_tap_done = sem("tap_done")
        s_u_ready = sem("u_ready")
        s_z_ready = sem("z_ready")
        s_xp_mm = sem("xp_mm")
        s_xdbl_ready = sem("xdbl_ready")
        s_bc_stored = sem("bc_stored")
        s_dt_mm = sem("dt_mm")
        s_vpos_ready = sem("vpos_ready")
        s_vabs_ready = sem("vabs_ready")
        s_vln_ready = sem("vln_ready")
        s_dt_sum = sem("dt_sum")
        s_dtu_ready = sem("dtu_ready")
        s_dt_ready = sem("dt_ready")
        s_da_ready = sem("da_ready")
        s_dbu_ready = sem("dbu_ready")
        s_scan_done = sem("scan_done")
        s_hc_ready = sem("hc_ready")
        s_y_acc = sem("y_acc")
        s_y1_done = sem("y1_done")
        s_yg_ready = sem("yg_ready")
        s_out_mm = sem("out_mm")
        s_gated = sem("gated")
        s_x1_ready = sem("x1_ready")
        s_st1_ready = sem("st1_ready")
        s_ve1_ready = sem("ve1_ready")
        s_rs1_ready = sem("rs1_ready")
        s_xh_ready = sem("xh_ready")
        s_x1T_mm = sem("x1T_mm")
        s_xT_ready = sem("xT_ready")
        s_q_mm = sem("q_mm")
        s_k_mm = sem("k_mm")
        s_v_mm = sem("v_mm")
        s_qmax_ready = sem("qmax_ready")
        s_qsub_ready = sem("qsub_ready")
        s_qe_ready = sem("qe_ready")
        s_kmax_ready = sem("kmax_ready")
        s_ke_ready = sem("ke_ready")
        s_v_ready = sem("v_ready")
        s_qrec_step = sem("qrec_step")
        s_krec_ready = sem("krec_ready")
        s_qT_mm = sem("qT_mm")
        s_kT_mm = sem("kT_mm")
        s_qT_ready = sem("qT_ready")
        s_kT_ready = sem("kT_ready")
        s_att_mm = sem("att_mm")
        s_att_ready = sem("att_ready")
        s_y_mm = sem("y_mm")
        s_yq_ready = sem("yq_ready")
        s_st2_ready = sem("st2_ready")
        s_ve2_ready = sem("ve2_ready")
        s_rs2_ready = sem("rs2_ready")
        s_yh_ready = sem("yh_ready")
        s_yT_mm = sem("yT_mm")
        s_hT_ready = sem("hT_ready")
        s_o_mm = sem("o_mm")
        s_fin_ready = sem("fin_ready")
        x_loaded = [sem(f"x_loaded{i}") for i in range(XBUF)]
        bc_loaded = [sem(f"bc_loaded{i}") for i in range(2)]
        s_out_stored = sem("out_stored")

        def pcol(name, lo=0, hi=None):
            s, e = COLS[name]
            return par[:, s + lo:(e if hi is None else s + hi)]

        def over_batches(col):
            return col.unsqueeze(2).to_broadcast([P, col.shape[1], NB])

        block = ctx.enter_context(nc.Block())

        @block.sync
        def _(sp):
            def load_x(b):
                if b >= XBUF:
                    sp.wait_ge(s_x1_ready, b - XBUF + 1)
                sp.dma_start(xg[:, b % XBUF], a["x"][b].rearrange("(c p) d -> p c d", p=P)).then_inc(
                    x_loaded[b % XBUF], 16)

            def broadcast_bc(b):
                if b >= 2:
                    sp.wait_ge(s_dbu_ready, U * (b - 1))
                    sp.wait_ge(s_hc_ready, U * (b - 1))
                if b == 1:
                    sp.wait_ge(s_mod_mm, 2)
                sp.wait_ge(s_xdbl_ready, b + 1)
                sp.dma_start(bc_dram[b % 2], xdbl[RANK:RANK + 2 * N, :]).then_inc(s_bc_stored, 16)
                sp.wait_ge(s_bc_stored, 16 * (b + 1))
                sp.dma_start(BC[:, b % 2], bc_dram[b % 2].unsqueeze(0).to_broadcast([P, 2 * N, T])).then_inc(
                    bc_loaded[b % 2], 16)

            def store(b):
                sp.wait_ge(s_fin_ready, b + 1)
                sp.dma_start(out[b].rearrange("(c p) d -> p c d", p=P), fin[:, :, :]).then_inc(s_out_stored, 16)

            sp.dma_start(cT[:, :, :], a["cT"].rearrange("(k p) b -> p k b", p=P)).then_inc(s_ld_par, 16)
            sp.dma_start(par[:, :], a["par"]).then_inc(s_ld_par, 16)
            sp.dma_start(ident[:, :], a["ident"]).then_inc(s_ld_par, 16)
            load_x(0)
            sp.dma_start(adaT, a["ada_wT"].rearrange("(k p) (s e) -> p k s e", p=P, e=D)).then_inc(s_ld_ada, 16)
            sp.dma_start(win[:, :, :], a["in_wT"].rearrange("(k p) e -> p k e", p=P)).then_inc(s_ld_win, 16)
            sp.dma_start(embT, a["W_emb"].rearrange("(k p) (s e) -> p k s e", p=P, e=D)).then_inc(s_ld_ada, 16)
            sp.dma_start(wxp[:, :, :], a["xp_wT"].rearrange("(k p) e -> p k e", p=P)).then_inc(s_ld_w, 16)
            sp.dma_start(wdt[:, :], a["dt_wT"]).then_inc(s_ld_w, 16)
            load_x(1)
            sp.dma_start(gb8[:, :], a["ada_b"][2 * D:3 * D].unsqueeze(0).to_broadcast([NB, D])).then_inc(s_ld_small, 16)
            sp.wait_ge(s_pool_const, 1)
            sp.dma_start(krhs[32:33, :], a["mask_row"]).then_inc(s_ld_small, 16)
            sp.dma_start(klhs[0:1, :], a["bk"].unsqueeze(0)).then_inc(s_ld_small, 16)
            broadcast_bc(0)
            sp.dma_start(wo[:, :, :], a["out_wT"].rearrange("(k p) e -> p k e", p=P)).then_inc(s_ld_post, 16)
            for i, w in enumerate(("Wq", "Wk", "Wv", "W_out")):
                sp.dma_start(wqkvo[:, i], a[w].rearrange("(k p) e -> p k e", p=P)).then_inc(s_ld_post, 16)
            for i, w in enumerate(("bq", "bv", "b_out")):
                sp.dma_start(brow[:, i, :], a[w].unsqueeze(0)).then_inc(s_ld_post, 16)
            sp.dma_start(blockmask[:, :], a["blockmask"]).then_inc(s_ld_post, 16)
            for b in range(NB):
                if b + 2 < NB:
                    load_x(b + 2)
                if b + 1 < NB:
                    broadcast_bc(b + 1)
                if b >= 1:
                    store(b - 1)
            store(NB - 1)
            sp.wait_ge(s_out_stored, 16 * NB)

        @block.gpsimd
        def _(pool):
            nc.gpsimd.memset(klhs[:, :], 0.0).then_inc(s_krow_ready, 1)
            nc.gpsimd.memset(krhs[:, :], 0.0).then_inc(s_krow_ready, 1)
            pool.wait_ge(s_krow_ready, 2)
            nc.gpsimd.memset(klhs[32:33, :], 1.0).then_inc(s_krow_ready, 1)
            nc.gpsimd.memset(krhs[0:1, :], 1.0).then_inc(s_krow_ready, 1)
            pool.wait_ge(s_krow_ready, 4)
            nc.gpsimd.memset(mhalf[:, :], -0.5).then_inc(s_pool_const, 1)

            def rstd(ready, b, mv, ve, rs, ve_sem, rs_sem):
                pool.wait_ge(ready, 2 * TC * (b + 1))
                nc.gpsimd.tensor_scalar(ve[:, :], mv[:, :, 1], EPS, None, ALU.add).then_inc(ve_sem, 1)
                pool.wait_ge(ve_sem, b + 1)
                nc.gpsimd.tensor_tensor(rs[:, :], ve[:, :], mhalf[:, :], ALU.pow).then_inc(rs_sem, 1)

            def rstd0(b):
                rstd(s_st0_ready, b, mv0, ve0, rs0, s_ve0_ready, s_rs0_ready)

            def softplus_sum(b):
                pool.wait_ge(s_vpos_ready, DC * (b + 1))
                pool.wait_ge(s_vln_ready, 2 * (b + 1))
                nc.gpsimd.tensor_tensor(dt[:, b % 2], dt[:, b % 2], vln[:, :, :], ALU.add).then_inc(s_dt_sum, 1)
                pool.wait_ge(s_dt_sum, b + 1)
                pool.wait_ge(s_u_ready, b + 1)
                nc.gpsimd.tensor_tensor(dtu[:, b % 2], dt[:, b % 2], u[:, b % 2], ALU.mult).then_inc(s_dtu_ready, 1)
                pool.wait_ge(s_dtu_ready, b + 1)
                nc.gpsimd.memset(dt[:, b % 2, :, 0:1], BIG).then_inc(s_dt_ready, 1)

            def inputs_of(b, i):
                g, dc, q = U * b + i, i // UPC, i % UPC
                if i == 0:
                    pool.wait_ge(bc_loaded[b % 2], 16 * (b // 2 + 1))
                if g >= DBUF:
                    pool.wait_ge(s_scan_done, g - DBUF + 1)
                nc.gpsimd.tensor_tensor(
                    dBu[:, g % DBUF], dtu[:, b % 2, dc, :].unsqueeze(1).to_broadcast([P, NQ, T]),
                    BC[:, b % 2, NQ * q:NQ * q + NQ, :], ALU.mult).then_inc(s_dbu_ready, 1)

            def residual(b):
                pool.wait_ge(s_gated, b + 1)
                nc.gpsimd.tensor_tensor(x1[:, :, :], x1[:, :, :], xg[:, b % XBUF], ALU.add).then_inc(s_x1_ready, 1)

            rstd0(0)
            softplus_sum(0)
            for b in range(NB):
                for i in range(U):
                    inputs_of(b, i)
                    if b >= 1:
                        if i == POOL_SLOT["residual"]:
                            residual(b - 1)
                        if i == POOL_SLOT["rstd1"]:
                            rstd(s_st1_ready, b - 1, mv1, ve1, rs1, s_ve1_ready, s_rs1_ready)
                        if i == POOL_SLOT["rstd2"]:
                            rstd(s_st2_ready, b - 1, mv2, ve2, rs2, s_ve2_ready, s_rs2_ready)
                    if b + 1 < NB:
                        if i == POOL_SLOT["rstd0"]:
                            rstd0(b + 1)
                        if i == POOL_SLOT["softplus"]:
                            softplus_sum(b + 1)
            residual(NB - 1)
            rstd(s_st1_ready, NB - 1, mv1, ve1, rs1, s_ve1_ready, s_rs1_ready)
            rstd(s_st2_ready, NB - 1, mv2, ve2, rs2, s_ve2_ready, s_rs2_ready)

        @block.scalar
        def _(act):
            def setup():
                act.wait_ge(s_ld_par, 48)
                nc.scalar.activation(cT[:, :, :], cT[:, :, :], ACT.Silu).then_inc(s_sc_ready, 1)
                nc.scalar.activation(Aneg[:, :], pcol("A_log"), ACT.Exp).then_inc(s_aexp_ready, 1)

            def modulated(b):
                act.wait_ge(s_xT_mm, b + 1)
                if b == 0:
                    act.wait_ge(s_m0_ready, 8)
                for k in range(KD):
                    nc.scalar.activation(xnT[:, k, :], PX[:, k, :], ACT.Identity, bias=m0b[:, k, b:b + 1],
                                         scale=m0s[:, k, b:b + 1]).then_inc(s_xn_ready, 1)

            def conv_last_tap(b, h):
                act.wait_ge(s_xz_mm, 4 * b + h + 1)
                if b >= 1:
                    act.wait_ge(s_dt_sum, b)
                for e in range(2):
                    dc = 2 * h + e
                    nc.scalar.activation(conv[:, dc, :], PX[:, e, :], ACT.Identity, bias=pcol("conv_b", dc, dc + 1),
                                         scale=pcol("conv_w", TAPS * dc + 3, TAPS * dc + 4)).then_inc(s_conv0_ready, 1)

            def silu_z(b, h):
                act.wait_ge(s_xz_mm, 4 * b + 3 + h)
                if b >= 2:
                    act.wait_ge(s_yg_ready, DC * (b - 1))
                nc.scalar.activation(zs[:, b % 2, 2 * h:2 * h + 2, :], PX[:, :, :], ACT.Silu).then_inc(s_z_ready, 1)

            def silu_u(b):
                act.wait_ge(s_tap_done, 3 * DC * (b + 1))
                if b >= 2:
                    act.wait_ge(s_y1_done, DC * (b - 1))
                nc.scalar.activation(u[:, b % 2], conv[:, :, :], ACT.Silu).then_inc(s_u_ready, 1)

            def copy_xdbl(b):
                act.wait_ge(s_xp_mm, b + 1)
                if b >= 1:
                    act.wait_ge(s_bc_stored, 16 * b)
                nc.scalar.activation(xdbl[:, :], PX[0:RANK + 2 * N, 0, :], ACT.Copy).then_inc(s_xdbl_ready, 1)

            def abs_dt(b, h):
                act.wait_ge(s_vpos_ready, DC * b + 2 * h + 2)
                act.wait_ge(s_u_ready, b + 1)
                for e in range(2):
                    dc = 2 * h + e
                    nc.scalar.activation(vln[:, dc, :], PX[:, e, :], ACT.Abs,
                                         bias=pcol("dt_b", dc, dc + 1)).then_inc(s_vabs_ready, 1)

            def log_dt(b):
                act.wait_ge(s_vabs_ready, DC * (b + 1))
                nc.scalar.activation(vln[:, :, :], vln[:, :, :], ACT.Exp, scale=-1.0).then_inc(s_vln_ready, 1)
                act.wait_ge(s_vln_ready, 2 * b + 1)
                nc.scalar.activation(vln[:, :, :], vln[:, :, :], ACT.Ln, bias=1.0).then_inc(s_vln_ready, 1)

            def decays(b, i):
                g, dc, q = U * b + i, i // UPC, i % UPC
                if i == 0:
                    act.wait_ge(s_dt_ready, b + 1)
                if g == 0:
                    act.wait_ge(s_aneg_ready, 1)
                    act.wait_ge(s_gate_ready, 1)
                if g >= 2:
                    act.wait_ge(s_hc_ready, g - 1)
                for j in range(NQ):
                    c = N * dc + NQ * q + j
                    ins = nc.scalar.activation(ring[:, g % 2, j, :], dt[:, b % 2, dc, :], ACT.Exp,
                                               scale=Aneg[:, c:c + 1])
                ins.then_inc(s_da_ready, 1)

            def norm1(b):
                act.wait_ge(s_x1T_mm, b + 1)
                for k in range(KD):
                    nc.scalar.activation(xT[:, k, :], PZ[:, k, :], ACT.Identity, bias=pcol("ln1_b", k, k + 1),
                                         scale=pcol("ln1_w", k, k + 1)).then_inc(s_xT_ready, 1)

            def exp_qk(b):
                act.wait_ge(s_qsub_ready, b + 1)
                nc.scalar.activation(qe[:, :, :], qe[:, :, :], ACT.Exp).then_inc(s_qe_ready, 1)
                act.wait_ge(s_kmax_ready, 2 * (b + 1))
                for k in range(KD):
                    nc.scalar.activation(ke[:, k, :], PZ[:, k, :], ACT.Exp, bias=kmax[:, k:k + 1],
                                         accum_out=ksum[:, k:k + 1]).then_inc(s_ke_ready, 1)

            def mask_v(b):
                act.wait_ge(s_v_mm, b + 1)
                for c in range(TC):
                    nc.scalar.activation(vm[:, c, :], PY[:, c, :], ACT.Copy,
                                         scale=pcol("mask", TC * b + c, TC * b + c + 1)).then_inc(s_v_ready, 1)

            def copy_qT(b):
                act.wait_ge(s_qT_mm, b + 1)
                nc.scalar.activation(qT[:, :, :], PZ[:, :, :], ACT.Copy).then_inc(s_qT_ready, 1)

            def silu_h(b):
                act.wait_ge(s_yT_mm, b + 1)
                for k in range(KD):
                    nc.scalar.activation(xT[:, k, :], PZ[:, k, :], ACT.Silu, bias=m1b[:, k, b:b + 1],
                                         scale=m1s[:, k, b:b + 1]).then_inc(s_hT_ready, 1)

            PRE = [modulated, lambda b: conv_last_tap(b, 0), lambda b: conv_last_tap(b, 1), lambda b: silu_z(b, 0),
                   lambda b: silu_z(b, 1), silu_u, copy_xdbl, lambda b: abs_dt(b, 0), lambda b: abs_dt(b, 1), log_dt]
            POST = [norm1, exp_qk, mask_v, copy_qT, silu_h]
            setup()
            for step in PRE:
                step(0)
            for b in range(NB):
                for i in range(U):
                    decays(b, i)
                    if b + 1 < NB:
                        for s, step in zip(ACT_PRE, PRE):
                            if s == i:
                                step(b + 1)
                    if b >= 1:
                        for s, step in zip(ACT_POST, POST):
                            if s == i:
                                step(b - 1)
            for step in POST:
                step(NB - 1)

        @block.vector
        def _(dve):
            V = nc.vector

            def stats(b, src, st, mv, ready):
                for c in range(TC):
                    V.bn_stats(st[:, c, :], src[:, c, :]).then_inc(ready, 1)
                for c in range(TC):
                    dve.wait_ge(ready, 2 * TC * b + TC)
                    V.bn_aggr(mv[:, c, :], st[:, c, :]).then_inc(ready, 1)

            def normalize(dst, src, mv, rs, ready):
                for c in range(TC):
                    V.tensor_scalar(dst[:, c, :], src[:, c, :], mv[:, c, 0:1], rs[:, c:c + 1], ALU.subtract,
                                    ALU.mult).then_inc(ready, 1)

            def stats0(b):
                dve.wait_ge(x_loaded[b % XBUF], 16 * (b // XBUF + 1))
                if b >= 1:
                    dve.wait_ge(s_ve0_ready, b)
                stats(b, xg[:, b % XBUF], st0, mv0, s_st0_ready)

            def normalize0(b):
                dve.wait_ge(s_rs0_ready, b + 1)
                if b >= 1:
                    dve.wait_ge(s_xT_mm, b)
                normalize(xhat, xg[:, b % XBUF], mv0, rs0, s_xhat_ready)

            def conv_taps(b, h):
                dve.wait_ge(s_conv0_ready, DC * b + 2 * h + 2)
                for s in range(1, TAPS):
                    for e in range(2):
                        dc = 2 * h + e
                        if s > 1:
                            dve.wait_ge(s_tap_done, 3 * DC * b + 6 * h + 2 * (s - 2) + e + 1)
                        w = pcol("conv_w", TAPS * dc + 3 - s, TAPS * dc + 4 - s)
                        V.scalar_tensor_tensor(conv[:, dc, s:], PX[:, e, 0:T - s], w, conv[:, dc, s:], ALU.mult,
                                               ALU.add).then_inc(s_tap_done, 1)

            def relu_dt(b, h):
                dve.wait_ge(s_dt_mm, 2 * b + h + 1)
                if b >= 2:
                    dve.wait_ge(s_da_ready, U * (b - 1))
                for e in range(2):
                    dc = 2 * h + e
                    V.tensor_scalar(dt[:, b % 2, dc, :], PX[:, e, :], pcol("dt_b", dc, dc + 1), 0.0, ALU.add,
                                    ALU.max).then_inc(s_vpos_ready, 1)

            def scan_unit(b, i):
                g = U * b + i
                q = i % UPC
                dve.wait_ge(s_da_ready, g + 1)
                dve.wait_ge(s_dbu_ready, g + 1)
                states = ring[:, g % 2].rearrange("p n t -> p (n t)")
                V.tensor_tensor_scan(states, states, dBu[:, g % DBUF].rearrange("p n t -> p (n t)"), 0.0, ALU.mult,
                                     ALU.add).then_inc(s_scan_done, 1)
                dve.wait_ge(s_scan_done, g + 1)
                if i == 0:
                    dve.wait_ge(bc_loaded[b % 2], 16 * (b // 2 + 1))
                if g >= HBUF:
                    dve.wait_ge(s_y_acc, g - HBUF + 1)
                V.tensor_tensor(hC[:, g % HBUF], ring[:, g % 2], BC[:, b % 2, N + NQ * q:N + NQ * q + NQ, :],
                                ALU.mult).then_inc(s_hc_ready, 1)

            def skip_term(b, dc):
                dve.wait_ge(s_y_acc, U * b + UPC * (dc + 1))
                if b >= 1 and dc == 0:
                    dve.wait_ge(s_out_mm, b)
                V.scalar_tensor_tensor(yg[:, dc, :], u[:, b % 2, dc, :], pcol("D_par", dc, dc + 1), YB[:, :],
                                       ALU.mult, ALU.add).then_inc(s_y1_done, 1)

            def gate_y(b, dc):
                dve.wait_ge(s_y1_done, DC * b + dc + 1)
                V.tensor_tensor(yg[:, dc, :], yg[:, dc, :], zs[:, b % 2, dc, :], ALU.mult).then_inc(s_yg_ready, 1)

            def gate_x(b):
                dve.wait_ge(s_out_mm, b + 1)
                if b >= 1:
                    dve.wait_ge(s_fin_ready, b)
                V.tensor_tensor(x1[:, :, :], PY[:, :, :], gate[:, b, :].unsqueeze(1).to_broadcast([P, TC, D]),
                                ALU.mult).then_inc(s_gated, 1)

            def stats1(b):
                dve.wait_ge(s_x1_ready, b + 1)
                stats(b, x1, st1, mv1, s_st1_ready)

            def normalize1(b):
                dve.wait_ge(s_rs1_ready, b + 1)
                if b >= 1:
                    dve.wait_ge(s_yT_mm, b)
                normalize(xh, x1, mv1, rs1, s_xh_ready)

            def max_qk(b):
                dve.wait_ge(s_q_mm, b + 1)
                heads = PY[:, :, :].rearrange("p c (h e) -> p (c h) e", h=HEADS)
                V.tensor_reduce(qmax[:, :, :].rearrange("p c h -> p (c h)"), heads, AX.X,
                                ALU.max).then_inc(s_qmax_ready, 1)
                dve.wait_ge(s_k_mm, b + 1)
                V.tensor_reduce(kmax[:, :], PZ[:, :, :], AX.X, ALU.max).then_inc(s_kmax_ready, 1)
                dve.wait_ge(s_qmax_ready, b + 1)
                V.tensor_tensor(qe[:, :, :].rearrange("p c (h e) -> p (c h) e", h=HEADS), heads,
                                qmax[:, :, :].rearrange("p c h -> p (c h)").unsqueeze(2).to_broadcast(
                                    [P, TC * HEADS, DH]), ALU.subtract).then_inc(s_qsub_ready, 1)
                dve.wait_ge(s_kmax_ready, 2 * b + 1)
                V.tensor_scalar(kmax[:, :], kmax[:, :], -1.0, None, ALU.mult).then_inc(s_kmax_ready, 1)

            def sums_qk(b):
                dve.wait_ge(s_qe_ready, b + 1)
                V.tensor_reduce(qsum[:, :, :].rearrange("p c h -> p (c h)"),
                                qe[:, :, :].rearrange("p c (h e) -> p (c h) e", h=HEADS), AX.X,
                                ALU.add).then_inc(s_qrec_step, 1)
                dve.wait_ge(s_ke_ready, KD * (b + 1))
                V.reciprocal(rk[:, :], ksum[:, :]).then_inc(s_krec_ready, 1)
                dve.wait_ge(s_qrec_step, 2 * b + 1)
                V.reciprocal(rq[:, :, :], qsum[:, :, :]).then_inc(s_qrec_step, 1)

            def copy_kT(b):
                dve.wait_ge(s_kT_mm, b + 1)
                V.tensor_copy(kT[:, :, :], PY[:, :, :]).then_inc(s_kT_ready, 1)

            def head_blocks(b):
                dve.wait_ge(s_att_mm, b + 1)
                dve.wait_ge(s_krec_ready, b + 1)
                for k in range(KD):
                    V.scalar_tensor_tensor(att[:, k, :], PZ[:, 0, P * k:P * k + P], rk[:, k:k + 1], blockmask[:, :],
                                           ALU.mult, ALU.mult).then_inc(s_att_ready, 1)

            def normalize_q(b):
                dve.wait_ge(s_y_mm, b + 1)
                dve.wait_ge(s_qrec_step, 2 * b + 2)
                dve.wait_ge(s_qT_mm, b + 1)
                V.tensor_tensor(yq[:, :, :].rearrange("p c (h e) -> p (c h) e", h=HEADS),
                                PY[:, :, :].rearrange("p c (h e) -> p (c h) e", h=HEADS),
                                rq[:, :, :].rearrange("p c h -> p (c h)").unsqueeze(2).to_broadcast(
                                    [P, TC * HEADS, DH]), ALU.mult).then_inc(s_yq_ready, 1)

            def stats2(b):
                dve.wait_ge(s_yq_ready, b + 1)
                stats(b, yq, st2, mv2, s_st2_ready)

            def normalize2(b):
                dve.wait_ge(s_rs2_ready, b + 1)
                dve.wait_ge(s_x1T_mm, b + 1)
                normalize(xh, yq, mv2, rs2, s_yh_ready)

            def finish(b):
                dve.wait_ge(s_o_mm, b + 1)
                if b >= 1:
                    dve.wait_ge(s_out_stored, 16 * b)
                V.tensor_tensor(fin[:, :, :], PY[:, :, :], x1[:, :, :], ALU.add).then_inc(s_fin_ready, 1)

            def setup():
                dve.wait_ge(s_aexp_ready, 1)
                V.tensor_scalar(Aneg[:, :], Aneg[:, :], -1.0, -1e-30, ALU.mult, ALU.min).then_inc(s_aneg_ready, 1)
                dve.wait_ge(s_mod_mm, 1)
                pm = PX[:, 0, 0:4 * KD * NB].rearrange("p (j b) -> p j b", b=NB)
                V.tensor_tensor(mods[:, 0:2 * KD, :], pm[:, 0:2 * KD, :], over_batches(pcol("ada_b")),
                                ALU.add).then_inc(s_mod_ready, 1)
                V.tensor_tensor(mods[:, 2 * KD:4 * KD, :], pm[:, 2 * KD:4 * KD, :], over_batches(pcol("emb_b")),
                                ALU.add).then_inc(s_mod_ready, 1)
                dve.wait_ge(s_mod_ready, 2)
                shift0, scale0 = mods[:, 0:KD, :], mods[:, KD:2 * KD, :]
                scale1, shift1 = mods[:, 2 * KD:3 * KD, :], mods[:, 3 * KD:4 * KD, :]
                for k in range(KD):
                    for dst, src, w in ((m0s, scale0, "ln_g"), (m0b, scale0, "ln_b"), (m1s, scale1, "ln2_w"),
                                        (m1b, scale1, "ln2_b")):
                        V.tensor_scalar(dst[:, k, :], src[:, k, :], 1.0, pcol(w, k, k + 1), ALU.add,
                                        ALU.mult).then_inc(s_mod_ready, 1)
                dve.wait_ge(s_mod_ready, 2 + 4 * KD)
                for k in range(KD):
                    for s, dst, src in ((m0s, m0b, shift0), (m1s, m1b, shift1)):
                        V.tensor_tensor(dst[:, k, :], dst[:, k, :], src[:, k, :], ALU.add).then_inc(s_m0_ready, 2)

            def setup_gate():
                dve.wait_ge(s_mod_mm, 2)
                dve.wait_ge(s_ld_small, 48)
                V.tensor_tensor(gate8[:, :], PY[0:NB, 0, :], gb8[:, :], ALU.add).then_inc(s_gate8_ready, 1)
                V.tensor_scalar(krhs[32:33, :], krhs[32:33, :], -1.0, MASKED, ALU.add, ALU.mult).then_inc(s_krow_ready, 1)
                dve.wait_ge(s_gate_mm, 1)
                V.tensor_copy(gate[:, :, :], ring[:, :, :, :].rearrange("p r n t -> p (r n) t")).then_inc(s_gate_ready, 1)

            PRE = [stats0, normalize0, lambda b: conv_taps(b, 0), lambda b: conv_taps(b, 1),
                   lambda b: relu_dt(b, 0), lambda b: relu_dt(b, 1)]
            POST = [gate_x, stats1, normalize1, max_qk, sums_qk, copy_kT, head_blocks, normalize_q, stats2,
                    normalize2, finish]
            PRE[0](0)
            setup()
            PRE[1](0)
            setup_gate()
            for step in PRE[2:]:
                step(0)
            for b in range(NB):
                for i in range(U):
                    scan_unit(b, i)
                    if i % UPC == 0 and i > 0:
                        skip_term(b, i // UPC - 1)
                    if i % UPC == 1 and i > UPC:
                        gate_y(b, i // UPC - 1)
                    if b + 1 < NB:
                        for s, step in zip(DVE_PRE, PRE):
                            if s == i:
                                step(b + 1)
                    if b >= 1:
                        for s, step in zip(DVE_POST, POST):
                            if s == i:
                                step(b - 1)
                skip_term(b, DC - 1)
                gate_y(b, DC - 1)
            for step in POST:
                step(NB - 1)

        @block.tensor
        def _(pe):
            M = nc.tensor.matmul

            def transposes(dst, src):
                for k in range(2):
                    for c in range(2):
                        ins = nc.tensor.transpose(dst[:, k, P * c:P * c + P], src[:, c, P * k:P * k + P], ident[:, :])
                return ins

            def setup_mods():
                pe.wait_ge(s_sc_ready, 1)
                pe.wait_ge(s_ld_ada, 32)
                pm = PX[:, 0, 0:4 * KD * NB].rearrange("p (j b) -> p j b", b=NB)
                for j in range(4 * KD):
                    for k in range(KC):
                        w = adaT[:, k, j // KD] if j < 2 * KD else embT[:, k, j // KD - 2]
                        ins = M(pm[:, j, :], w[:, P * (j % KD):P * (j % KD) + P], cT[:, k, :], start=(k == 0),
                                stop=(k == KC - 1))
                ins.then_inc(s_mod_mm, 1)
                for k in range(KC):
                    ins = M(PY[0:NB, 0, :], cT[:, k, :], adaT[:, k, 2], start=(k == 0), stop=(k == KC - 1))
                ins.then_inc(s_mod_mm, 1)

            def setup_gate():
                pe.wait_ge(s_gate8_ready, 1)
                for b in range(NB):
                    ins = M(ring[:, b // NQ, b % NQ, :], ident[0:NB, b:b + 1].to_broadcast([NB, P]), gate8[:, :],
                            start=True, stop=True)
                ins.then_inc(s_gate_mm, 1)

            def transpose_x(b):
                pe.wait_ge(s_xhat_ready, TC * (b + 1))
                if b == 0:
                    pe.wait_ge(s_mod_ready, 2)
                if b >= 1:
                    pe.wait_ge(s_vpos_ready, DC * b)
                    pe.wait_ge(s_vabs_ready, DC * b)
                transposes(PX, xhat).then_inc(s_xT_mm, 1)

            def in_proj(b, h):
                if h == 0:
                    pe.wait_ge(s_xn_ready, KD * (b + 1))
                    if b == 0:
                        pe.wait_ge(s_ld_win, 16)
                elif h <= 2:
                    pe.wait_ge(s_tap_done, 3 * DC * b + 6 * h)
                else:
                    pe.wait_ge(s_z_ready, 2 * b + 1)
                for e in range(2):
                    lo = P * (2 * h + e)
                    for k in range(KD):
                        ins = M(PX[:, e, :], win[:, k, lo:lo + P], xnT[:, k, :], start=(k == 0), stop=(k == KD - 1))
                ins.then_inc(s_xz_mm, 1)

            def x_proj(b):
                pe.wait_ge(s_z_ready, 2 * b + 2)
                pe.wait_ge(s_u_ready, b + 1)
                if b == 0:
                    pe.wait_ge(s_ld_w, 32)
                for k in range(DC):
                    ins = M(PX[0:RANK + 2 * N, 0, :], wxp[:, k, :], u[:, b % 2, k, :], start=(k == 0),
                            stop=(k == DC - 1))
                ins.then_inc(s_xp_mm, 1)

            def dt_proj(b, h):
                if h == 0:
                    pe.wait_ge(s_xdbl_ready, b + 1)
                else:
                    pe.wait_ge(s_vpos_ready, DC * b + 2)
                    pe.wait_ge(s_vabs_ready, DC * b + 2)
                for e in range(2):
                    lo = P * (2 * h + e)
                    ins = M(PX[:, e, :], wdt[:, lo:lo + P], xdbl[0:RANK, :], start=True, stop=True)
                ins.then_inc(s_dt_mm, 1)

            def sum_states(b, i):
                g, dc, q = U * b + i, i // UPC, i % UPC
                pe.wait_ge(s_hc_ready, g + 1)
                if q == 0 and DC * b + dc >= 1:
                    pe.wait_ge(s_y1_done, DC * b + dc)
                for j in range(NQ):
                    ins = M(YB[:, :], ident[:, :], hC[:, g % HBUF, j, :], start=(q == 0 and j == 0),
                            stop=(q == UPC - 1 and j == NQ - 1))
                ins.then_inc(s_y_acc, 1)

            def out_proj(b):
                if b == 0:
                    pe.wait_ge(s_ld_post, 16 * 9)
                    pe.wait_ge(s_krow_ready, 5)
                    pe.wait_ge(s_gate8_ready, 1)
                else:
                    pe.wait_ge(s_fin_ready, b)
                pe.wait_ge(s_yg_ready, DC * (b + 1))
                for c in range(TC):
                    for k in range(DC):
                        ins = M(PY[:, c, :], yg[:, k, P * c:P * c + P], wo[:, k, :], start=(k == 0),
                                stop=(k == DC - 1))
                ins.then_inc(s_out_mm, 1)

            def transpose_x1(b):
                pe.wait_ge(s_xh_ready, TC * (b + 1))
                if b >= 1:
                    pe.wait_ge(s_hT_ready, KD * b)
                transposes(PZ, xh).then_inc(s_x1T_mm, 1)

            def rows(dst, w, bias):
                for c in range(TC):
                    for k in range(KD):
                        M(dst[:, c, :], xT[:, k, P * c:P * c + P], wqkvo[:, w, k, :], start=(k == 0), stop=False)
                    ins = M(dst[:, c, :], krhs[0:1, 0:P], brow[:, bias, :], start=False, stop=True)
                return ins

            def q_and_k(b):
                pe.wait_ge(s_xT_ready, KD * (b + 1))
                pe.wait_ge(s_gated, b + 1)
                rows(PY, 0, 0).then_inc(s_q_mm, 1)
                for h in range(KD):
                    for k in range(KD):
                        M(PZ[:, h, :], wqkvo[:, 1, k, P * h:P * h + P], xT[:, k, :], start=(k == 0), stop=False)
                    ins = M(PZ[:, h, :], klhs[:, P * h:P * h + P], krhs[:, T * b:T * b + T], start=False, stop=True)
                ins.then_inc(s_k_mm, 1)

            def v_rows(b):
                pe.wait_ge(s_qsub_ready, b + 1)
                rows(PY, 2, 1).then_inc(s_v_mm, 1)

            def transpose_qk(b):
                pe.wait_ge(s_qe_ready, b + 1)
                pe.wait_ge(s_ke_ready, KD * (b + 1))
                transposes(PZ, qe).then_inc(s_qT_mm, 1)
                pe.wait_ge(s_v_ready, TC * (b + 1))
                transposes(PY, ke).then_inc(s_kT_mm, 1)

            def k_times_v(b):
                pe.wait_ge(s_kT_ready, b + 1)
                pe.wait_ge(s_qT_ready, b + 1)
                for h in range(KD):
                    for c in range(TC):
                        ins = M(PZ[:, 0, P * h:P * h + P], kT[:, c, P * h:P * h + P], vm[:, c, P * h:P * h + P],
                                start=(c == 0), stop=(c == TC - 1))
                ins.then_inc(s_att_mm, 1)

            def q_times_att(b):
                pe.wait_ge(s_att_ready, KD * (b + 1))
                for c in range(TC):
                    for h in range(KD):
                        ins = M(PY[:, c, P * h:P * h + P], qT[:, h, P * c:P * c + P], att[:, h, :], start=True,
                                stop=True)
                ins.then_inc(s_y_mm, 1)

            def transpose_y(b):
                pe.wait_ge(s_yh_ready, TC * (b + 1))
                transposes(PZ, xh).then_inc(s_yT_mm, 1)

            def output(b):
                pe.wait_ge(s_hT_ready, KD * (b + 1))
                pe.wait_ge(s_yq_ready, b + 1)
                rows(PY, 3, 2).then_inc(s_o_mm, 1)

            PRE = [transpose_x, lambda b: in_proj(b, 0), lambda b: in_proj(b, 1), lambda b: in_proj(b, 2),
                   lambda b: in_proj(b, 3), x_proj, lambda b: dt_proj(b, 0), lambda b: dt_proj(b, 1)]
            POST = [out_proj, transpose_x1, q_and_k, v_rows, transpose_qk, k_times_v, q_times_att, transpose_y, output]
            setup_mods()
            transpose_x(0)
            setup_gate()
            for step in PRE[1:]:
                step(0)
            for b in range(NB):
                for i in range(U):
                    sum_states(b, i)
                    if b + 1 < NB:
                        for s, step in zip(PE_PRE, PRE):
                            if s == i:
                                step(b + 1)
                    if b >= 1:
                        for s, step in zip(PE_POST, POST):
                            if s == i:
                                step(b - 1)
            for step in POST:
                step(NB - 1)


POOL_SLOT = {"residual": 1, "rstd1": 2, "rstd2": 11, "rstd0": 0, "softplus": 10}
ACT_PRE = [1, 2, 3, 4, 5, 5, 6, 8, 9, 9]
ACT_POST = [3, 5, 6, 7, 13]
DVE_PRE = [0, 1, 3, 4, 8, 9]
DVE_POST = [1, 2, 3, 5, 7, 8, 9, 10, 11, 12, 14]
PE_PRE = [1, 2, 3, 4, 5, 6, 7, 8]
PE_POST = [0, 3, 4, 5, 6, 8, 9, 12, 13]


def kernel(x, cond_2048, mask_BxSx1_fk1, L0_cond_ln_g, L0_cond_ln_b, L0_cond_ada_w, L0_cond_ada_b, L0_cond_in_proj_w,
           L0_cond_conv_w, L0_cond_conv_b, L0_cond_x_proj_w, L0_cond_dt_proj_w, L0_cond_dt_proj_b, L0_cond_A_log,
           L0_cond_D_param, L0_cond_out_proj_w, L1_cond_ln_w, L1_cond_ln_b, L1_cond_Wq, L1_cond_bq, L1_cond_Wk,
           L1_cond_bk, L1_cond_Wv, L1_cond_bv, L1_cond_W_emb, L1_cond_b_emb, L1_cond_ln2_w, L1_cond_ln2_b,
           L1_cond_W_out, L1_cond_b_out):
    import numpy as np
    import concourse.bacc as bacc
    from concourse.bass_utils import run_bass_kernel_spmd

    def cols(v):
        v = np.asarray(v)
        v = v.reshape(v.shape[0] // P, P, -1)
        return v.transpose(1, 0, 2).reshape(P, -1)

    par = np.concatenate([
        cols(L0_cond_A_log), cols(L0_cond_conv_w), cols(L0_cond_conv_b), cols(L0_cond_dt_proj_b), cols(L0_cond_D_param),
        cols(L0_cond_ln_g), cols(L0_cond_ln_b), cols(np.asarray(L0_cond_ada_b)[:2 * D]), cols(L1_cond_b_emb),
        cols(L1_cond_ln_w), cols(L1_cond_ln_b), cols(L1_cond_ln2_w), cols(L1_cond_ln2_b),
        cols(np.asarray(mask_BxSx1_fk1).reshape(-1))], axis=1)
    heads = np.arange(P) // DH
    arrays = {
        "x": x, "cT": np.asarray(cond_2048).T, "par": par, "ident": np.eye(P, dtype=np.float32),
        "blockmask": (heads[:, None] == heads[None, :]).astype(np.float32), "ada_wT": np.asarray(L0_cond_ada_w).T,
        "ada_b": L0_cond_ada_b, "in_wT": np.asarray(L0_cond_in_proj_w).T, "xp_wT": np.asarray(L0_cond_x_proj_w).T,
        "dt_wT": np.asarray(L0_cond_dt_proj_w).T, "out_wT": np.asarray(L0_cond_out_proj_w).T, "Wq": L1_cond_Wq,
        "Wk": L1_cond_Wk, "Wv": L1_cond_Wv, "W_out": L1_cond_W_out, "bq": L1_cond_bq, "bk": L1_cond_bk,
        "bv": L1_cond_bv, "b_out": L1_cond_b_out, "W_emb": L1_cond_W_emb,
        "mask_row": np.asarray(mask_BxSx1_fk1).reshape(1, -1),
    }
    arrays = {k: np.ascontiguousarray(v) for k, v in arrays.items()}
    nc = bacc.Bacc("TRN2", target_bir_lowering=False, num_devices=1)
    aps = {k: nc.dram_tensor(f"in_{k}", v.shape, mybir.dt.from_np(v.dtype), kind="ExternalInput").ap()
           for k, v in arrays.items()}
    out = nc.dram_tensor("out", (NB, T, D), F32, kind="ExternalOutput").ap()
    build(nc, aps, out)
    r = run_bass_kernel_spmd(nc, [{f"in_{k}": v for k, v in arrays.items()}], core_ids=[0])
    return r.results[0]["out"]
```

```python
from contextlib import ExitStack

import concourse.bass as bass
from concourse import mybir

F32 = mybir.dt.float32
ALU = mybir.AluOpType
ACT = mybir.ActivationFunctionType
AX = mybir.AxisListType

P = 128
NB, T, D, DI, N = 8, 256, 256, 512, 16
RANK, TAPS, HEADS = 64, 4, 8
DH = D // HEADS
KC = 512 // P
KD = D // P
DC = DI // P
TC = T // P
NQ = 4
UPC = N // NQ
U = DC * UPC
NU = NQ * T
EPS = 1e-5
BIG = 1e37
MASKED = 1e6
DBUF, HBUF, XBUF = 3, 2, 3

COLS = {}
_at = 0
for _name, _n in (("A_log", DC * N), ("conv_w", DC * TAPS), ("conv_b", DC), ("dt_b", DC), ("D_par", DC), ("ln_g", KD),
                  ("ln_b", KD), ("ada_b", 2 * KD), ("emb_b", 2 * KD), ("ln1_w", KD), ("ln1_b", KD), ("ln2_w", KD),
                  ("ln2_b", KD), ("mask", NB * TC)):
    COLS[_name] = (_at, _at + _n)
    _at += _n
NPAR = _at


FIRST, LAST = -24, NB * U + 24


def due(g, slot):
    b, at = divmod(g - slot, U)
    return b if at == 0 and 0 <= b < NB else None


def build(nc, a, out):
    ctx = ExitStack()
    with ctx:
        def sb(name, shape):
            return ctx.enter_context(nc.sbuf_tensor(name, shape, F32))

        def ps(name, shape):
            return ctx.enter_context(nc.psum_tensor(name, shape, F32))

        def sem(name):
            return ctx.enter_context(nc.semaphore(name))

        par = sb("par", [P, NPAR])
        ident = sb("ident", [P, P])
        blockmask = sb("blockmask", [P, P])
        cT = sb("cT", [P, KC, NB])
        win = sb("win", [P, KD, 2 * DI])
        wxp = sb("wxp", [P, DC, RANK + 2 * N])
        wdt = sb("wdt", [RANK, DI])
        wo = sb("wo", [P, DC, D])
        wqkvo = sb("wqkvo", [P, 4, KD, D])
        klhs = sb("klhs", [33, D])
        krhs = sb("krhs", [33, NB * T])
        brow = sb("brow", [1, 3, D])
        gb8 = sb("gb8", [NB, D])
        gate8 = sb("gate8", [NB, D])
        gate = sb("gate", [P, NB, D])
        mods = sb("mods", [P, 4 * KD, NB])
        m0s, m0b = sb("m0s", [P, KD, NB]), sb("m0b", [P, KD, NB])
        m1s, m1b = sb("m1s", [P, KD, NB]), sb("m1b", [P, KD, NB])
        Aneg = sb("Aneg", [P, DC * N])
        mhalf = sb("mhalf", [P, TC])
        xg = sb("xg", [P, XBUF, TC, D])
        st0, mv0 = sb("st0", [P, TC, 6]), sb("mv0", [P, TC, 2])
        ve0, rs0 = sb("ve0", [P, TC]), sb("rs0", [P, TC])
        xhat = sb("xhat", [P, TC, D])
        xnT = sb("xnT", [P, KD, T])
        u = sb("u", [P, 2, DC, T])
        zs = sb("zs", [P, 2, DC, T])
        xdbl = sb("xdbl", [RANK + 2 * N, T])
        conv = sb("conv", [P, DC, T])
        vln = conv
        dt, dtu = sb("dt", [P, 2, DC, T]), sb("dtu", [P, 2, DC, T])
        BC = sb("BC", [P, 2, 2 * N, T])
        dBu = sb("dBu", [P, DBUF, NQ, T])
        hC = sb("hC", [P, HBUF, NQ, T])
        yg = sb("yg", [P, DC, T])
        x1 = sb("x1", [P, 2, TC, D])
        st1, mv1 = sb("st1", [P, TC, 6]), sb("mv1", [P, TC, 2])
        ve1, rs1 = sb("ve1", [P, TC]), sb("rs1", [P, TC])
        xh = sb("xh", [P, TC, D])
        xT = sb("xT", [P, KD, T])
        qmax, qsum, rq = sb("qmax", [P, TC, HEADS]), sb("qsum", [P, TC, HEADS]), sb("rq", [P, TC, HEADS])
        qe = sb("qe", [P, TC, D])
        kmax, ksum, rk = sb("kmax", [P, KD]), sb("ksum", [P, KD]), sb("rk", [P, KD])
        ke = sb("ke", [P, KD, T])
        vm = sb("vm", [P, TC, D])
        qT, kT = sb("qT", [P, KD, T]), sb("kT", [P, TC, D])
        att = sb("att", [P, KD, P])
        yq = qe
        st2, mv2 = sb("st2", [P, TC, 6]), sb("mv2", [P, TC, 2])
        ve2, rs2 = sb("ve2", [P, TC]), sb("rs2", [P, TC])
        fin = sb("fin", [P, TC, D])
        bc_dram = nc.dram_tensor("bc_rows", (2, 2 * N, T), F32, kind="Internal").ap()

        ring = ps("ring", [P, 2, NQ, T])
        YB = ps("YB", [P, T])
        PX = ps("PX", [P, 2, T])
        PY = ps("PY", [P, 2, T])
        PZ = ps("PZ", [P, 2, T])

        adaT = BC[:, 1, 0:3 * KC, :].rearrange("p (k s) e -> p k s e", k=KC)
        embT = BC[:, 1, 3 * KC:5 * KC, :].rearrange("p (k s) e -> p k s e", k=KC)

        s_ld_par = sem("ld_par")
        s_ld_ada = sem("ld_ada")
        s_ld_win = sem("ld_win")
        s_ld_small = sem("ld_small")
        s_ld_w = sem("ld_w")
        s_ld_post = sem("ld_post")
        s_pool_const = sem("pool_const")
        s_sc_ready = sem("sc_ready")
        s_aexp_ready = sem("aexp_ready")
        s_aneg_ready = sem("aneg_ready")
        s_mod_mm = sem("mod_mm")
        s_mod_ready = sem("mod_ready")
        s_m0_ready = sem("m0_ready")
        s_gate8_ready = sem("gate8_ready")
        s_gate_mm = sem("gate_mm")
        s_gate_ready = sem("gate_ready")
        s_krow_ready = sem("krow_ready")
        s_st0_ready = sem("st0_ready")
        s_ve0_ready = sem("ve0_ready")
        s_rs0_ready = sem("rs0_ready")
        s_xhat_ready = sem("xhat_ready")
        s_xT_mm = sem("xT_mm")
        s_xn_ready = sem("xn_ready")
        s_xz_mm = sem("xz_mm")
        s_conv0_ready = sem("conv0_ready")
        s_tap_done = sem("tap_done")
        s_u_ready = sem("u_ready")
        s_z_ready = sem("z_ready")
        s_xp_mm = sem("xp_mm")
        s_xdbl_ready = sem("xdbl_ready")
        s_bc_stored = sem("bc_stored")
        s_dt_mm = sem("dt_mm")
        s_vpos_ready = sem("vpos_ready")
        s_vabs_ready = sem("vabs_ready")
        s_vln_ready = sem("vln_ready")
        s_dt_sum = sem("dt_sum")
        s_dtu_ready = sem("dtu_ready")
        s_dt_ready = sem("dt_ready")
        s_da_ready = sem("da_ready")
        s_dbu_ready = sem("dbu_ready")
        s_scan_done = sem("scan_done")
        s_hc_ready = sem("hc_ready")
        s_y_acc = sem("y_acc")
        s_y1_done = sem("y1_done")
        s_yg_ready = sem("yg_ready")
        s_out_mm = sem("out_mm")
        s_gated = sem("gated")
        s_x1_ready = sem("x1_ready")
        s_st1_ready = sem("st1_ready")
        s_ve1_ready = sem("ve1_ready")
        s_rs1_ready = sem("rs1_ready")
        s_xh_ready = sem("xh_ready")
        s_x1T_mm = sem("x1T_mm")
        s_xT_ready = sem("xT_ready")
        s_q_mm = sem("q_mm")
        s_k_mm = sem("k_mm")
        s_v_mm = sem("v_mm")
        s_qmax_ready = sem("qmax_ready")
        s_qsub_ready = sem("qsub_ready")
        s_qe_ready = sem("qe_ready")
        s_kmax_ready = sem("kmax_ready")
        s_ke_ready = sem("ke_ready")
        s_v_ready = sem("v_ready")
        s_qrec_step = sem("qrec_step")
        s_krec_ready = sem("krec_ready")
        s_qT_mm = sem("qT_mm")
        s_kT_mm = sem("kT_mm")
        s_qT_ready = sem("qT_ready")
        s_kT_ready = sem("kT_ready")
        s_att_mm = sem("att_mm")
        s_att_ready = sem("att_ready")
        s_y_mm = sem("y_mm")
        s_yq_ready = sem("yq_ready")
        s_st2_ready = sem("st2_ready")
        s_ve2_ready = sem("ve2_ready")
        s_rs2_ready = sem("rs2_ready")
        s_yh_ready = sem("yh_ready")
        s_yT_mm = sem("yT_mm")
        s_hT_ready = sem("hT_ready")
        s_o_mm = sem("o_mm")
        s_fin_ready = sem("fin_ready")
        x_loaded = [sem(f"x_loaded{i}") for i in range(XBUF)]
        bc_loaded = [sem(f"bc_loaded{i}") for i in range(2)]
        s_out_stored = sem("out_stored")

        def pcol(name, lo=0, hi=None):
            s, e = COLS[name]
            return par[:, s + lo:(e if hi is None else s + hi)]

        def over_batches(col):
            return col.unsqueeze(2).to_broadcast([P, col.shape[1], NB])

        block = ctx.enter_context(nc.Block())

        @block.sync
        def _(sp):
            def load_x(b):
                if b >= XBUF:
                    sp.wait_ge(s_x1_ready, b - XBUF + 1)
                sp.dma_start(xg[:, b % XBUF], a["x"][b].rearrange("(c p) d -> p c d", p=P)).then_inc(
                    x_loaded[b % XBUF], 16)

            def broadcast_bc(b):
                if b >= 2:
                    sp.wait_ge(s_dbu_ready, U * (b - 1))
                    sp.wait_ge(s_hc_ready, U * (b - 1))
                if b == 1:
                    sp.wait_ge(s_mod_mm, 2)
                sp.wait_ge(s_xdbl_ready, b + 1)
                sp.dma_start(bc_dram[b % 2], xdbl[RANK:RANK + 2 * N, :]).then_inc(s_bc_stored, 16)
                sp.wait_ge(s_bc_stored, 16 * (b + 1))
                sp.dma_start(BC[:, b % 2], bc_dram[b % 2].unsqueeze(0).to_broadcast([P, 2 * N, T])).then_inc(
                    bc_loaded[b % 2], 16)

            def store(b):
                sp.wait_ge(s_fin_ready, b + 1)
                sp.dma_start(out[b].rearrange("(c p) d -> p c d", p=P), fin[:, :, :]).then_inc(s_out_stored, 16)

            sp.dma_start(cT[:, :, :], a["cT"].rearrange("(k p) b -> p k b", p=P)).then_inc(s_ld_par, 16)
            sp.dma_start(par[:, :], a["par"]).then_inc(s_ld_par, 16)
            sp.dma_start(ident[:, :], a["ident"]).then_inc(s_ld_par, 16)
            load_x(0)
            sp.dma_start(adaT, a["ada_wT"].rearrange("(k p) (s e) -> p k s e", p=P, e=D)).then_inc(s_ld_ada, 16)
            sp.dma_start(win[:, :, :], a["in_wT"].rearrange("(k p) e -> p k e", p=P)).then_inc(s_ld_win, 16)
            sp.dma_start(embT, a["W_emb"].rearrange("(k p) (s e) -> p k s e", p=P, e=D)).then_inc(s_ld_ada, 16)
            sp.dma_start(wxp[:, :, :], a["xp_wT"].rearrange("(k p) e -> p k e", p=P)).then_inc(s_ld_w, 16)
            sp.dma_start(wdt[:, :], a["dt_wT"]).then_inc(s_ld_w, 16)
            load_x(1)
            sp.dma_start(gb8[:, :], a["ada_b"][2 * D:3 * D].unsqueeze(0).to_broadcast([NB, D])).then_inc(s_ld_small, 16)
            sp.wait_ge(s_pool_const, 1)
            sp.dma_start(krhs[32:33, :], a["mask_row"]).then_inc(s_ld_small, 16)
            sp.dma_start(klhs[0:1, :], a["bk"].unsqueeze(0)).then_inc(s_ld_small, 16)
            broadcast_bc(0)
            sp.dma_start(wo[:, :, :], a["out_wT"].rearrange("(k p) e -> p k e", p=P)).then_inc(s_ld_post, 16)
            for i, w in enumerate(("Wq", "Wk", "Wv", "W_out")):
                sp.dma_start(wqkvo[:, i], a[w].rearrange("(k p) e -> p k e", p=P)).then_inc(s_ld_post, 16)
            for i, w in enumerate(("bq", "bv", "b_out")):
                sp.dma_start(brow[:, i, :], a[w].unsqueeze(0)).then_inc(s_ld_post, 16)
            sp.dma_start(blockmask[:, :], a["blockmask"]).then_inc(s_ld_post, 16)
            load_x(2)
            for b in range(1, NB + 3):
                if b < NB:
                    broadcast_bc(b)
                if b >= 3:
                    store(b - 3)
                if b + 2 < NB:
                    load_x(b + 2)
            sp.wait_ge(s_out_stored, 16 * NB)

        @block.gpsimd
        def _(pool):
            nc.gpsimd.memset(klhs[:, :], 0.0).then_inc(s_krow_ready, 1)
            nc.gpsimd.memset(krhs[:, :], 0.0).then_inc(s_krow_ready, 1)
            pool.wait_ge(s_krow_ready, 2)
            nc.gpsimd.memset(klhs[32:33, :], 1.0).then_inc(s_krow_ready, 1)
            nc.gpsimd.memset(krhs[0:1, :], 1.0).then_inc(s_krow_ready, 1)
            pool.wait_ge(s_krow_ready, 4)
            nc.gpsimd.memset(mhalf[:, :], -0.5).then_inc(s_pool_const, 1)

            def rstd(ready, b, mv, ve, rs, ve_sem, rs_sem):
                pool.wait_ge(ready, 2 * TC * (b + 1))
                nc.gpsimd.tensor_scalar(ve[:, :], mv[:, :, 1], EPS, None, ALU.add).then_inc(ve_sem, 1)
                pool.wait_ge(ve_sem, b + 1)
                nc.gpsimd.tensor_tensor(rs[:, :], ve[:, :], mhalf[:, :], ALU.pow).then_inc(rs_sem, 1)

            def rstd0(b):
                rstd(s_st0_ready, b, mv0, ve0, rs0, s_ve0_ready, s_rs0_ready)

            def softplus_sum(b):
                pool.wait_ge(s_vpos_ready, DC * (b + 1))
                pool.wait_ge(s_vln_ready, 2 * (b + 1))
                nc.gpsimd.tensor_tensor(dt[:, b % 2], dt[:, b % 2], vln[:, :, :], ALU.add).then_inc(s_dt_sum, 1)
                pool.wait_ge(s_dt_sum, b + 1)
                pool.wait_ge(s_u_ready, b + 1)
                nc.gpsimd.tensor_tensor(dtu[:, b % 2], dt[:, b % 2], u[:, b % 2], ALU.mult).then_inc(s_dtu_ready, 1)
                pool.wait_ge(s_dtu_ready, b + 1)
                nc.gpsimd.memset(dt[:, b % 2, :, 0:1], BIG).then_inc(s_dt_ready, 1)

            def inputs_of(b, i):
                g, dc, q = U * b + i, i // UPC, i % UPC
                if i == 0:
                    pool.wait_ge(bc_loaded[b % 2], 16 * (b // 2 + 1))
                if g >= DBUF:
                    pool.wait_ge(s_scan_done, g - DBUF + 1)
                nc.gpsimd.tensor_tensor(
                    dBu[:, g % DBUF], dtu[:, b % 2, dc, :].unsqueeze(1).to_broadcast([P, NQ, T]),
                    BC[:, b % 2, NQ * q:NQ * q + NQ, :], ALU.mult).then_inc(s_dbu_ready, 1)

            def residual(b):
                pool.wait_ge(s_gated, b + 1)
                nc.gpsimd.tensor_tensor(x1[:, b % 2], x1[:, b % 2], xg[:, b % XBUF], ALU.add).then_inc(s_x1_ready, 1)

            def rstd1(b):
                rstd(s_st1_ready, b, mv1, ve1, rs1, s_ve1_ready, s_rs1_ready)

            def rstd2(b):
                rstd(s_st2_ready, b, mv2, ve2, rs2, s_ve2_ready, s_rs2_ready)

            for g in range(FIRST, LAST):
                if 0 <= g < NB * U:
                    inputs_of(g // U, g % U)
                for slot, step in ((-20, rstd0), (-3, softplus_sum), (22, residual), (23, rstd1), (36, rstd2)):
                    b = due(g, slot)
                    if b is not None:
                        step(b)

        @block.scalar
        def _(act):
            def setup():
                act.wait_ge(s_ld_par, 48)
                nc.scalar.activation(cT[:, :, :], cT[:, :, :], ACT.Silu).then_inc(s_sc_ready, 1)
                nc.scalar.activation(Aneg[:, :], pcol("A_log"), ACT.Exp).then_inc(s_aexp_ready, 1)

            def modulated(b):
                act.wait_ge(s_xT_mm, b + 1)
                if b == 0:
                    act.wait_ge(s_m0_ready, 8)
                for k in range(KD):
                    nc.scalar.activation(xnT[:, k, :], PX[:, k, :], ACT.Identity, bias=m0b[:, k, b:b + 1],
                                         scale=m0s[:, k, b:b + 1]).then_inc(s_xn_ready, 1)

            def conv_last_tap(b, h):
                act.wait_ge(s_xz_mm, 4 * b + h + 1)
                if b >= 1:
                    act.wait_ge(s_dt_sum, b)
                for e in range(2):
                    dc = 2 * h + e
                    nc.scalar.activation(conv[:, dc, :], PX[:, e, :], ACT.Identity, bias=pcol("conv_b", dc, dc + 1),
                                         scale=pcol("conv_w", TAPS * dc + 3, TAPS * dc + 4)).then_inc(s_conv0_ready, 1)

            def copy_z(b):
                act.wait_ge(s_xz_mm, 4 * b + 3)
                if b >= 2:
                    act.wait_ge(s_yg_ready, DC * (b - 1))
                nc.scalar.activation(zs[:, b % 2, 0:2, :], PX[:, :, :], ACT.Copy).then_inc(s_z_ready, 1)

            def silu_z(b):
                act.wait_ge(s_z_ready, 3 * b + 1)
                nc.scalar.activation(zs[:, b % 2, 0:2, :], zs[:, b % 2, 0:2, :], ACT.Silu).then_inc(s_z_ready, 1)
                act.wait_ge(s_xz_mm, 4 * b + 4)
                nc.scalar.activation(zs[:, b % 2, 2:4, :], PX[:, :, :], ACT.Silu).then_inc(s_z_ready, 1)

            def silu_u(b):
                act.wait_ge(s_tap_done, 3 * DC * (b + 1))
                if b >= 2:
                    act.wait_ge(s_y1_done, DC * (b - 1))
                nc.scalar.activation(u[:, b % 2], conv[:, :, :], ACT.Silu).then_inc(s_u_ready, 1)

            def copy_xdbl(b):
                act.wait_ge(s_xp_mm, b + 1)
                if b >= 1:
                    act.wait_ge(s_bc_stored, 16 * b)
                nc.scalar.activation(xdbl[:, :], PX[0:RANK + 2 * N, 0, :], ACT.Copy).then_inc(s_xdbl_ready, 1)

            def abs_dt(b, h):
                act.wait_ge(s_vpos_ready, DC * b + 2 * h + 2)
                act.wait_ge(s_u_ready, b + 1)
                for e in range(2):
                    dc = 2 * h + e
                    nc.scalar.activation(vln[:, dc, :], PX[:, e, :], ACT.Abs,
                                         bias=pcol("dt_b", dc, dc + 1)).then_inc(s_vabs_ready, 1)

            def log_dt(b):
                act.wait_ge(s_vabs_ready, DC * (b + 1))
                nc.scalar.activation(vln[:, :, :], vln[:, :, :], ACT.Exp, scale=-1.0).then_inc(s_vln_ready, 1)
                act.wait_ge(s_vln_ready, 2 * b + 1)
                nc.scalar.activation(vln[:, :, :], vln[:, :, :], ACT.Ln, bias=1.0).then_inc(s_vln_ready, 1)

            def decays(b, i):
                g, dc, q = U * b + i, i // UPC, i % UPC
                if i == 0:
                    act.wait_ge(s_dt_ready, b + 1)
                if g == 0:
                    act.wait_ge(s_aneg_ready, 1)
                    act.wait_ge(s_gate_ready, 1)
                if g >= 2:
                    act.wait_ge(s_hc_ready, g - 1)
                for j in range(NQ):
                    c = N * dc + NQ * q + j
                    ins = nc.scalar.activation(ring[:, g % 2, j, :], dt[:, b % 2, dc, :], ACT.Exp,
                                               scale=Aneg[:, c:c + 1])
                ins.then_inc(s_da_ready, 1)

            def norm1(b):
                act.wait_ge(s_x1T_mm, b + 1)
                if b >= 1:
                    act.wait_ge(s_o_mm, b)
                for k in range(KD):
                    nc.scalar.activation(xT[:, k, :], PZ[:, k, :], ACT.Identity, bias=pcol("ln1_b", k, k + 1),
                                         scale=pcol("ln1_w", k, k + 1)).then_inc(s_xT_ready, 1)

            def exp_qk(b):
                act.wait_ge(s_qsub_ready, b + 1)
                nc.scalar.activation(qe[:, :, :], qe[:, :, :], ACT.Exp).then_inc(s_qe_ready, 1)
                act.wait_ge(s_kmax_ready, 2 * (b + 1))
                for k in range(KD):
                    nc.scalar.activation(ke[:, k, :], PZ[:, k, :], ACT.Exp, bias=kmax[:, k:k + 1],
                                         accum_out=ksum[:, k:k + 1]).then_inc(s_ke_ready, 1)

            def mask_v(b):
                act.wait_ge(s_v_mm, b + 1)
                for c in range(TC):
                    nc.scalar.activation(vm[:, c, :], PY[:, c, :], ACT.Copy,
                                         scale=pcol("mask", TC * b + c, TC * b + c + 1)).then_inc(s_v_ready, 1)

            def copy_qT(b):
                act.wait_ge(s_qT_mm, b + 1)
                nc.scalar.activation(qT[:, :, :], PZ[:, :, :], ACT.Copy).then_inc(s_qT_ready, 1)

            def silu_h(b):
                act.wait_ge(s_yT_mm, b + 1)
                for k in range(KD):
                    nc.scalar.activation(xT[:, k, :], PZ[:, k, :], ACT.Silu, bias=m1b[:, k, b:b + 1],
                                         scale=m1s[:, k, b:b + 1]).then_inc(s_hT_ready, 1)

            def conv_last_tap_0(b):
                conv_last_tap(b, 0)

            def conv_last_tap_1(b):
                conv_last_tap(b, 1)

            def abs_dt_0(b):
                abs_dt(b, 0)

            def abs_dt_1(b):
                abs_dt(b, 1)

            def silus(b):
                if b < NB:
                    silu_z(b)
                    silu_u(b)
                if b >= 3:
                    silu_h(b - 3)
                nc.scalar.preload_act_table_set("natural_log_exp_and_others")

            setup()
            for g in range(FIRST, LAST):
                if 0 <= g < NB * U:
                    decays(g // U, g % U)
                for slot, step in ((-19, modulated), (-18, conv_last_tap_0), (-16, conv_last_tap_1), (-14, copy_z),
                                   (-9, copy_xdbl), (-7, abs_dt_0), (-5, abs_dt_1), (-5, log_dt), (24, norm1),
                                   (27, exp_qk), (29, mask_v), (31, copy_qT)):
                    b = due(g, slot)
                    if b is not None:
                        step(b)
                if (g + 11) % U == 0 and 0 <= (g + 11) // U < NB + 3:
                    silus((g + 11) // U)

        @block.vector
        def _(dve):
            V = nc.vector

            def stats(b, src, st, mv, ready):
                for c in range(TC):
                    V.bn_stats(st[:, c, :], src[:, c, :]).then_inc(ready, 1)
                for c in range(TC):
                    dve.wait_ge(ready, 2 * TC * b + TC)
                    V.bn_aggr(mv[:, c, :], st[:, c, :]).then_inc(ready, 1)

            def normalize(dst, src, mv, rs, ready):
                for c in range(TC):
                    V.tensor_scalar(dst[:, c, :], src[:, c, :], mv[:, c, 0:1], rs[:, c:c + 1], ALU.subtract,
                                    ALU.mult).then_inc(ready, 1)

            def stats0(b):
                dve.wait_ge(x_loaded[b % XBUF], 16 * (b // XBUF + 1))
                if b >= 1:
                    dve.wait_ge(s_ve0_ready, b)
                stats(b, xg[:, b % XBUF], st0, mv0, s_st0_ready)

            def normalize0(b):
                dve.wait_ge(s_rs0_ready, b + 1)
                if b >= 1:
                    dve.wait_ge(s_xT_mm, b)
                normalize(xhat, xg[:, b % XBUF], mv0, rs0, s_xhat_ready)

            def conv_taps(b, h):
                dve.wait_ge(s_conv0_ready, DC * b + 2 * h + 2)
                for s in range(1, TAPS):
                    for e in range(2):
                        dc = 2 * h + e
                        if s > 1:
                            dve.wait_ge(s_tap_done, 3 * DC * b + 6 * h + 2 * (s - 2) + e + 1)
                        w = pcol("conv_w", TAPS * dc + 3 - s, TAPS * dc + 4 - s)
                        V.scalar_tensor_tensor(conv[:, dc, s:], PX[:, e, 0:T - s], w, conv[:, dc, s:], ALU.mult,
                                               ALU.add).then_inc(s_tap_done, 1)

            def relu_dt(b, h):
                dve.wait_ge(s_dt_mm, 2 * b + h + 1)
                if b >= 2:
                    dve.wait_ge(s_da_ready, U * (b - 1))
                for e in range(2):
                    dc = 2 * h + e
                    V.tensor_scalar(dt[:, b % 2, dc, :], PX[:, e, :], pcol("dt_b", dc, dc + 1), 0.0, ALU.add,
                                    ALU.max).then_inc(s_vpos_ready, 1)

            def scan_unit(b, i):
                g = U * b + i
                q = i % UPC
                dve.wait_ge(s_da_ready, g + 1)
                dve.wait_ge(s_dbu_ready, g + 1)
                states = ring[:, g % 2].rearrange("p n t -> p (n t)")
                V.tensor_tensor_scan(states, states, dBu[:, g % DBUF].rearrange("p n t -> p (n t)"), 0.0, ALU.mult,
                                     ALU.add).then_inc(s_scan_done, 1)
                dve.wait_ge(s_scan_done, g + 1)
                if i == 0:
                    dve.wait_ge(bc_loaded[b % 2], 16 * (b // 2 + 1))
                if g >= HBUF:
                    dve.wait_ge(s_y_acc, g - HBUF + 1)
                V.tensor_tensor(hC[:, g % HBUF], ring[:, g % 2], BC[:, b % 2, N + NQ * q:N + NQ * q + NQ, :],
                                ALU.mult).then_inc(s_hc_ready, 1)

            def skip_term(b, dc):
                dve.wait_ge(s_y_acc, U * b + UPC * (dc + 1))
                if b >= 1 and dc == 0:
                    dve.wait_ge(s_out_mm, b)
                V.scalar_tensor_tensor(yg[:, dc, :], u[:, b % 2, dc, :], pcol("D_par", dc, dc + 1), YB[:, :],
                                       ALU.mult, ALU.add).then_inc(s_y1_done, 1)

            def gate_y(b, dc):
                dve.wait_ge(s_y1_done, DC * b + dc + 1)
                V.tensor_tensor(yg[:, dc, :], yg[:, dc, :], zs[:, b % 2, dc, :], ALU.mult).then_inc(s_yg_ready, 1)

            def gate_x(b):
                dve.wait_ge(s_out_mm, b + 1)
                if b >= 2:
                    dve.wait_ge(s_fin_ready, b - 1)
                V.tensor_tensor(x1[:, b % 2], PY[:, :, :], gate[:, b, :].unsqueeze(1).to_broadcast([P, TC, D]),
                                ALU.mult).then_inc(s_gated, 1)

            def stats1(b):
                dve.wait_ge(s_x1_ready, b + 1)
                stats(b, x1[:, b % 2], st1, mv1, s_st1_ready)

            def normalize1(b):
                dve.wait_ge(s_rs1_ready, b + 1)
                if b >= 1:
                    dve.wait_ge(s_yT_mm, b)
                normalize(xh, x1[:, b % 2], mv1, rs1, s_xh_ready)

            def max_qk(b):
                dve.wait_ge(s_q_mm, b + 1)
                heads = PY[:, :, :].rearrange("p c (h e) -> p (c h) e", h=HEADS)
                V.tensor_reduce(qmax[:, :, :].rearrange("p c h -> p (c h)"), heads, AX.X,
                                ALU.max).then_inc(s_qmax_ready, 1)
                dve.wait_ge(s_k_mm, b + 1)
                V.tensor_reduce(kmax[:, :], PZ[:, :, :], AX.X, ALU.max).then_inc(s_kmax_ready, 1)
                dve.wait_ge(s_qmax_ready, b + 1)
                V.tensor_tensor(qe[:, :, :].rearrange("p c (h e) -> p (c h) e", h=HEADS), heads,
                                qmax[:, :, :].rearrange("p c h -> p (c h)").unsqueeze(2).to_broadcast(
                                    [P, TC * HEADS, DH]), ALU.subtract).then_inc(s_qsub_ready, 1)
                dve.wait_ge(s_kmax_ready, 2 * b + 1)
                V.tensor_scalar(kmax[:, :], kmax[:, :], -1.0, None, ALU.mult).then_inc(s_kmax_ready, 1)

            def sums_qk(b):
                dve.wait_ge(s_qe_ready, b + 1)
                V.tensor_reduce(qsum[:, :, :].rearrange("p c h -> p (c h)"),
                                qe[:, :, :].rearrange("p c (h e) -> p (c h) e", h=HEADS), AX.X,
                                ALU.add).then_inc(s_qrec_step, 1)
                dve.wait_ge(s_ke_ready, KD * (b + 1))
                V.reciprocal(rk[:, :], ksum[:, :]).then_inc(s_krec_ready, 1)
                dve.wait_ge(s_qrec_step, 2 * b + 1)
                V.reciprocal(rq[:, :, :], qsum[:, :, :]).then_inc(s_qrec_step, 1)

            def copy_kT(b):
                dve.wait_ge(s_kT_mm, b + 1)
                V.tensor_copy(kT[:, :, :], PY[:, :, :]).then_inc(s_kT_ready, 1)

            def head_blocks(b):
                dve.wait_ge(s_att_mm, b + 1)
                dve.wait_ge(s_krec_ready, b + 1)
                for k in range(KD):
                    V.scalar_tensor_tensor(att[:, k, :], PZ[:, 0, P * k:P * k + P], rk[:, k:k + 1], blockmask[:, :],
                                           ALU.mult, ALU.mult).then_inc(s_att_ready, 1)

            def normalize_q(b):
                dve.wait_ge(s_y_mm, b + 1)
                dve.wait_ge(s_qrec_step, 2 * b + 2)
                dve.wait_ge(s_qT_mm, b + 1)
                V.tensor_tensor(yq[:, :, :].rearrange("p c (h e) -> p (c h) e", h=HEADS),
                                PY[:, :, :].rearrange("p c (h e) -> p (c h) e", h=HEADS),
                                rq[:, :, :].rearrange("p c h -> p (c h)").unsqueeze(2).to_broadcast(
                                    [P, TC * HEADS, DH]), ALU.mult).then_inc(s_yq_ready, 1)

            def stats2(b):
                dve.wait_ge(s_yq_ready, b + 1)
                stats(b, yq, st2, mv2, s_st2_ready)

            def normalize2(b):
                dve.wait_ge(s_rs2_ready, b + 1)
                dve.wait_ge(s_x1T_mm, b + 1)
                normalize(xh, yq, mv2, rs2, s_yh_ready)

            def finish(b):
                dve.wait_ge(s_o_mm, b + 1)
                if b >= 1:
                    dve.wait_ge(s_out_stored, 16 * b)
                V.tensor_tensor(fin[:, :, :], PY[:, :, :], x1[:, b % 2], ALU.add).then_inc(s_fin_ready, 1)

            def setup():
                dve.wait_ge(s_aexp_ready, 1)
                V.tensor_scalar(Aneg[:, :], Aneg[:, :], -1.0, -1e-30, ALU.mult, ALU.min).then_inc(s_aneg_ready, 1)
                dve.wait_ge(s_mod_mm, 1)
                pm = PX[:, 0, 0:4 * KD * NB].rearrange("p (j b) -> p j b", b=NB)
                V.tensor_tensor(mods[:, 0:2 * KD, :], pm[:, 0:2 * KD, :], over_batches(pcol("ada_b")),
                                ALU.add).then_inc(s_mod_ready, 1)
                V.tensor_tensor(mods[:, 2 * KD:4 * KD, :], pm[:, 2 * KD:4 * KD, :], over_batches(pcol("emb_b")),
                                ALU.add).then_inc(s_mod_ready, 1)
                dve.wait_ge(s_mod_ready, 2)
                shift0, scale0 = mods[:, 0:KD, :], mods[:, KD:2 * KD, :]
                scale1, shift1 = mods[:, 2 * KD:3 * KD, :], mods[:, 3 * KD:4 * KD, :]
                for k in range(KD):
                    for dst, src, w in ((m0s, scale0, "ln_g"), (m0b, scale0, "ln_b"), (m1s, scale1, "ln2_w"),
                                        (m1b, scale1, "ln2_b")):
                        V.tensor_scalar(dst[:, k, :], src[:, k, :], 1.0, pcol(w, k, k + 1), ALU.add,
                                        ALU.mult).then_inc(s_mod_ready, 1)
                dve.wait_ge(s_mod_ready, 2 + 4 * KD)
                for k in range(KD):
                    for s, dst, src in ((m0s, m0b, shift0), (m1s, m1b, shift1)):
                        V.tensor_tensor(dst[:, k, :], dst[:, k, :], src[:, k, :], ALU.add).then_inc(s_m0_ready, 2)

            def setup_gate():
                dve.wait_ge(s_mod_mm, 2)
                dve.wait_ge(s_ld_small, 48)
                V.tensor_tensor(gate8[:, :], PY[0:NB, 0, :], gb8[:, :], ALU.add).then_inc(s_gate8_ready, 1)
                V.tensor_scalar(krhs[32:33, :], krhs[32:33, :], -1.0, MASKED, ALU.add, ALU.mult).then_inc(s_krow_ready, 1)
                dve.wait_ge(s_gate_mm, 1)
                V.tensor_copy(gate[:, :, :], ring[:, :, :, :].rearrange("p r n t -> p (r n) t")).then_inc(s_gate_ready, 1)

            def conv_taps_0(b):
                conv_taps(b, 0)

            def conv_taps_1(b):
                conv_taps(b, 1)

            def relu_dt_0(b):
                relu_dt(b, 0)

            def relu_dt_1(b):
                relu_dt(b, 1)

            for g in range(FIRST, LAST):
                if 0 <= g < NB * U:
                    scan_unit(g // U, g % U)
                for dc in range(DC):
                    b = due(g, UPC * (dc + 1))
                    if b is not None:
                        skip_term(b, dc)
                    b = due(g, UPC * (dc + 1) + 1)
                    if b is not None:
                        gate_y(b, dc)
                for slot, step in ((-23, stats0), (-22, normalize0), (-19, conv_taps_0), (-17, conv_taps_1),
                                   (-9, relu_dt_0), (-7, relu_dt_1), (19, gate_x), (20, stats1), (21, normalize1),
                                   (25, max_qk), (27, sums_qk), (29, copy_kT), (31, head_blocks), (32, normalize_q),
                                   (33, stats2), (34, normalize2), (38, finish)):
                    b = due(g, slot)
                    if b is not None:
                        step(b)
                if g == -23:
                    setup()
                if g == -22:
                    setup_gate()

        @block.tensor
        def _(pe):
            M = nc.tensor.matmul

            def transposes(dst, src):
                for k in range(2):
                    for c in range(2):
                        ins = nc.tensor.transpose(dst[:, k, P * c:P * c + P], src[:, c, P * k:P * k + P], ident[:, :])
                return ins

            def setup_mods():
                pe.wait_ge(s_sc_ready, 1)
                pe.wait_ge(s_ld_ada, 32)
                pm = PX[:, 0, 0:4 * KD * NB].rearrange("p (j b) -> p j b", b=NB)
                for j in range(4 * KD):
                    for k in range(KC):
                        w = adaT[:, k, j // KD] if j < 2 * KD else embT[:, k, j // KD - 2]
                        ins = M(pm[:, j, :], w[:, P * (j % KD):P * (j % KD) + P], cT[:, k, :], start=(k == 0),
                                stop=(k == KC - 1))
                ins.then_inc(s_mod_mm, 1)
                for k in range(KC):
                    ins = M(PY[0:NB, 0, :], cT[:, k, :], adaT[:, k, 2], start=(k == 0), stop=(k == KC - 1))
                ins.then_inc(s_mod_mm, 1)

            def setup_gate():
                pe.wait_ge(s_gate8_ready, 1)
                for b in range(NB):
                    ins = M(ring[:, b // NQ, b % NQ, :], ident[0:NB, b:b + 1].to_broadcast([NB, P]), gate8[:, :],
                            start=True, stop=True)
                ins.then_inc(s_gate_mm, 1)

            def transpose_x(b):
                pe.wait_ge(s_xhat_ready, TC * (b + 1))
                if b == 0:
                    pe.wait_ge(s_mod_ready, 2)
                if b >= 1:
                    pe.wait_ge(s_vpos_ready, DC * b)
                    pe.wait_ge(s_vabs_ready, DC * b)
                transposes(PX, xhat).then_inc(s_xT_mm, 1)

            def in_proj(b, h):
                if h == 0:
                    pe.wait_ge(s_xn_ready, KD * (b + 1))
                    if b == 0:
                        pe.wait_ge(s_ld_win, 16)
                elif h <= 2:
                    pe.wait_ge(s_tap_done, 3 * DC * b + 6 * h)
                else:
                    pe.wait_ge(s_z_ready, 3 * b + 1)
                for e in range(2):
                    lo = P * (2 * h + e)
                    for k in range(KD):
                        ins = M(PX[:, e, :], win[:, k, lo:lo + P], xnT[:, k, :], start=(k == 0), stop=(k == KD - 1))
                ins.then_inc(s_xz_mm, 1)

            def x_proj(b):
                pe.wait_ge(s_z_ready, 3 * b + 3)
                pe.wait_ge(s_u_ready, b + 1)
                if b == 0:
                    pe.wait_ge(s_ld_w, 32)
                for k in range(DC):
                    ins = M(PX[0:RANK + 2 * N, 0, :], wxp[:, k, :], u[:, b % 2, k, :], start=(k == 0),
                            stop=(k == DC - 1))
                ins.then_inc(s_xp_mm, 1)

            def dt_proj(b, h):
                if h == 0:
                    pe.wait_ge(s_xdbl_ready, b + 1)
                else:
                    pe.wait_ge(s_vpos_ready, DC * b + 2)
                    pe.wait_ge(s_vabs_ready, DC * b + 2)
                for e in range(2):
                    lo = P * (2 * h + e)
                    ins = M(PX[:, e, :], wdt[:, lo:lo + P], xdbl[0:RANK, :], start=True, stop=True)
                ins.then_inc(s_dt_mm, 1)

            def sum_states(b, i):
                g, dc, q = U * b + i, i // UPC, i % UPC
                pe.wait_ge(s_hc_ready, g + 1)
                if q == 0 and DC * b + dc >= 1:
                    pe.wait_ge(s_y1_done, DC * b + dc)
                for j in range(NQ):
                    ins = M(YB[:, :], ident[:, :], hC[:, g % HBUF, j, :], start=(q == 0 and j == 0),
                            stop=(q == UPC - 1 and j == NQ - 1))
                ins.then_inc(s_y_acc, 1)

            def out_proj(b):
                if b == 0:
                    pe.wait_ge(s_ld_post, 16 * 9)
                    pe.wait_ge(s_krow_ready, 5)
                    pe.wait_ge(s_gate8_ready, 1)
                else:
                    pe.wait_ge(s_yq_ready, b)
                pe.wait_ge(s_yg_ready, DC * (b + 1))
                for c in range(TC):
                    for k in range(DC):
                        ins = M(PY[:, c, :], yg[:, k, P * c:P * c + P], wo[:, k, :], start=(k == 0),
                                stop=(k == DC - 1))
                ins.then_inc(s_out_mm, 1)

            def transpose_x1(b):
                pe.wait_ge(s_xh_ready, TC * (b + 1))
                if b >= 1:
                    pe.wait_ge(s_hT_ready, KD * b)
                transposes(PZ, xh).then_inc(s_x1T_mm, 1)

            def rows(dst, w, bias):
                for c in range(TC):
                    for k in range(KD):
                        M(dst[:, c, :], xT[:, k, P * c:P * c + P], wqkvo[:, w, k, :], start=(k == 0), stop=False)
                    ins = M(dst[:, c, :], krhs[0:1, 0:P], brow[:, bias, :], start=False, stop=True)
                return ins

            def q_and_k(b):
                pe.wait_ge(s_xT_ready, KD * (b + 1))
                pe.wait_ge(s_gated, b + 1)
                if b >= 1:
                    pe.wait_ge(s_fin_ready, b)
                rows(PY, 0, 0).then_inc(s_q_mm, 1)
                for h in range(KD):
                    for k in range(KD):
                        M(PZ[:, h, :], wqkvo[:, 1, k, P * h:P * h + P], xT[:, k, :], start=(k == 0), stop=False)
                    ins = M(PZ[:, h, :], klhs[:, P * h:P * h + P], krhs[:, T * b:T * b + T], start=False, stop=True)
                ins.then_inc(s_k_mm, 1)

            def v_rows(b):
                pe.wait_ge(s_qsub_ready, b + 1)
                rows(PY, 2, 1).then_inc(s_v_mm, 1)

            def transpose_qk(b):
                pe.wait_ge(s_qe_ready, b + 1)
                pe.wait_ge(s_ke_ready, KD * (b + 1))
                transposes(PZ, qe).then_inc(s_qT_mm, 1)
                pe.wait_ge(s_v_ready, TC * (b + 1))
                transposes(PY, ke).then_inc(s_kT_mm, 1)

            def k_times_v(b):
                pe.wait_ge(s_kT_ready, b + 1)
                pe.wait_ge(s_qT_ready, b + 1)
                for h in range(KD):
                    for c in range(TC):
                        ins = M(PZ[:, 0, P * h:P * h + P], kT[:, c, P * h:P * h + P], vm[:, c, P * h:P * h + P],
                                start=(c == 0), stop=(c == TC - 1))
                ins.then_inc(s_att_mm, 1)

            def q_times_att(b):
                pe.wait_ge(s_att_ready, KD * (b + 1))
                for c in range(TC):
                    for h in range(KD):
                        ins = M(PY[:, c, P * h:P * h + P], qT[:, h, P * c:P * c + P], att[:, h, :], start=True,
                                stop=True)
                ins.then_inc(s_y_mm, 1)

            def transpose_y(b):
                pe.wait_ge(s_yh_ready, TC * (b + 1))
                transposes(PZ, xh).then_inc(s_yT_mm, 1)

            def output(b):
                pe.wait_ge(s_hT_ready, KD * (b + 1))
                pe.wait_ge(s_gated, min(b + 2, NB))
                rows(PY, 3, 2).then_inc(s_o_mm, 1)

            def in_proj_0(b):
                in_proj(b, 0)

            def in_proj_1(b):
                in_proj(b, 1)

            def in_proj_2(b):
                in_proj(b, 2)

            def in_proj_3(b):
                in_proj(b, 3)

            def dt_proj_0(b):
                dt_proj(b, 0)

            def dt_proj_1(b):
                dt_proj(b, 1)

            setup_mods()
            for g in range(FIRST, LAST):
                if 0 <= g < NB * U:
                    sum_states(g // U, g % U)
                for slot, step in ((-22, transpose_x), (-21, in_proj_0), (-19, in_proj_1), (-17, in_proj_2),
                                   (-15, in_proj_3), (-12, x_proj), (-10, dt_proj_0), (-8, dt_proj_1), (17, out_proj),
                                   (21, transpose_x1), (23, q_and_k), (26, v_rows), (28, transpose_qk),
                                   (30, k_times_v), (31, q_times_att), (34, transpose_y), (36, output)):
                    b = due(g, slot)
                    if b is not None:
                        step(b)
                if g == -22:
                    setup_gate()


def kernel(x, cond_2048, mask_BxSx1_fk1, L0_cond_ln_g, L0_cond_ln_b, L0_cond_ada_w, L0_cond_ada_b, L0_cond_in_proj_w,
           L0_cond_conv_w, L0_cond_conv_b, L0_cond_x_proj_w, L0_cond_dt_proj_w, L0_cond_dt_proj_b, L0_cond_A_log,
           L0_cond_D_param, L0_cond_out_proj_w, L1_cond_ln_w, L1_cond_ln_b, L1_cond_Wq, L1_cond_bq, L1_cond_Wk,
           L1_cond_bk, L1_cond_Wv, L1_cond_bv, L1_cond_W_emb, L1_cond_b_emb, L1_cond_ln2_w, L1_cond_ln2_b,
           L1_cond_W_out, L1_cond_b_out):
    import numpy as np
    import concourse.bacc as bacc
    from concourse.bass_utils import run_bass_kernel_spmd

    def cols(v):
        v = np.asarray(v)
        v = v.reshape(v.shape[0] // P, P, -1)
        return v.transpose(1, 0, 2).reshape(P, -1)

    par = np.concatenate([
        cols(L0_cond_A_log), cols(L0_cond_conv_w), cols(L0_cond_conv_b), cols(L0_cond_dt_proj_b), cols(L0_cond_D_param),
        cols(L0_cond_ln_g), cols(L0_cond_ln_b), cols(np.asarray(L0_cond_ada_b)[:2 * D]), cols(L1_cond_b_emb),
        cols(L1_cond_ln_w), cols(L1_cond_ln_b), cols(L1_cond_ln2_w), cols(L1_cond_ln2_b),
        cols(np.asarray(mask_BxSx1_fk1).reshape(-1))], axis=1)
    heads = np.arange(P) // DH
    arrays = {
        "x": x, "cT": np.asarray(cond_2048).T, "par": par, "ident": np.eye(P, dtype=np.float32),
        "blockmask": (heads[:, None] == heads[None, :]).astype(np.float32), "ada_wT": np.asarray(L0_cond_ada_w).T,
        "ada_b": L0_cond_ada_b, "in_wT": np.asarray(L0_cond_in_proj_w).T, "xp_wT": np.asarray(L0_cond_x_proj_w).T,
        "dt_wT": np.asarray(L0_cond_dt_proj_w).T, "out_wT": np.asarray(L0_cond_out_proj_w).T, "Wq": L1_cond_Wq,
        "Wk": L1_cond_Wk, "Wv": L1_cond_Wv, "W_out": L1_cond_W_out, "bq": L1_cond_bq, "bk": L1_cond_bk,
        "bv": L1_cond_bv, "b_out": L1_cond_b_out, "W_emb": L1_cond_W_emb,
        "mask_row": np.asarray(mask_BxSx1_fk1).reshape(1, -1),
    }
    arrays = {k: np.ascontiguousarray(v) for k, v in arrays.items()}
    nc = bacc.Bacc("TRN2", target_bir_lowering=False, num_devices=1)
    aps = {k: nc.dram_tensor(f"in_{k}", v.shape, mybir.dt.from_np(v.dtype), kind="ExternalInput").ap()
           for k, v in arrays.items()}
    out = nc.dram_tensor("out", (NB, T, D), F32, kind="ExternalOutput").ap()
    build(nc, aps, out)
    r = run_bass_kernel_spmd(nc, [{f"in_{k}": v for k, v in arrays.items()}], core_ids=[0])
    return r.results[0]["out"]
```

```python
from contextlib import ExitStack

import concourse.bass as bass
from concourse import mybir

F32 = mybir.dt.float32
BF16 = mybir.dt.bfloat16
ALU = mybir.AluOpType
ACT = mybir.ActivationFunctionType
AX = mybir.AxisListType

P = 128
NB, T, D, DI, N = 8, 256, 256, 512, 16
RANK, TAPS, HEADS = 64, 4, 8
DH = D // HEADS
KC = 512 // P
KD = D // P
DC = DI // P
TC = T // P
NQ = 4
UPC = N // NQ
U = DC * UPC
NU = NQ * T
EPS = 1e-5
BIG = 1e37
MASKED = 1e6
DBUF, XBUF = 5, 3
THIRDS = (0, 64, 96)
SPLIT = THIRDS[-1] + 1
ONES_ROW = RANK + 2 * N

COLS = {}
_at = 0
for _name, _n in (("A_log", DC * N), ("conv_w", DC * TAPS), ("conv_b", DC), ("D_par", DC), ("ln_g", KD),
                  ("ln_b", KD), ("ada_b", 2 * KD), ("emb_b", 2 * KD), ("ln1_w", KD), ("ln1_b", KD), ("ln2_w", KD),
                  ("ln2_b", KD), ("mask", NB * TC)):
    COLS[_name] = (_at, _at + _n)
    _at += _n
NPAR = _at


FIRST, LAST = -24, NB * U + 26


def due(g, slot):
    b, at = divmod(g - slot, U)
    return b if at == 0 and 0 <= b < NB else None


def build(nc, a, out):
    ctx = ExitStack()
    with ctx:
        def sb(name, shape):
            return ctx.enter_context(nc.sbuf_tensor(name, shape, F32))

        def sbb(name, shape):
            return ctx.enter_context(nc.sbuf_tensor(name, shape, BF16))

        def ps(name, shape):
            return ctx.enter_context(nc.psum_tensor(name, shape, F32))

        def sem(name):
            return ctx.enter_context(nc.semaphore(name))

        par = sb("par", [P, NPAR])
        ident = sb("ident", [P, P])
        blockmask = sb("blockmask", [P, P])
        cT = sb("cT", [P, KC, NB])
        win = sb("win", [P, KD, 2 * DI])
        wxp = sb("wxp", [P, DC, RANK + 2 * N])
        wdt = sb("wdt", [ONES_ROW + 1, DI])
        wo = sb("wo", [P, DC, D])
        wqkvo = sb("wqkvo", [P, 4, KD, D])
        ones3 = sbb("ones3", [SPLIT, T])
        rows3 = sbb("rows3", [SPLIT, 4 * D + NB * T])
        gb8 = sb("gb8", [NB, D])
        gate8 = sb("gate8", [NB, D])
        gate = sb("gate", [P, NB, D])
        mods = sb("mods", [P, 4 * KD, NB])
        m0s, m0b = sb("m0s", [P, KD, NB]), sb("m0b", [P, KD, NB])
        m1s, m1b = sb("m1s", [P, KD, NB]), sb("m1b", [P, KD, NB])
        Aneg = sb("Aneg", [P, DC * N])
        mhalf = sb("mhalf", [P, TC])
        xg = sb("xg", [P, XBUF, TC, D])
        st0, mv0 = sb("st0", [P, TC, 6]), sb("mv0", [P, TC, 2])
        ve0, rs0, nb0 = sb("ve0", [P, TC]), sb("rs0", [P, TC]), sb("nb0", [P, TC])
        xhat = sb("xhat", [P, TC, D])
        xnT = sb("xnT", [P, KD, T])
        u = sb("u", [P, 2, DC, T])
        zs = sb("zs", [P, 2, DC, T])
        xdbl = sb("xdbl", [ONES_ROW + 1, T])
        conv = sb("conv", [P, DC, T])
        vln = conv
        dt, dtu = sb("dt", [P, 2, DC, T]), sb("dtu", [P, 2, DC, T])
        BC = sb("BC", [P, 2, 2 * N, T])
        hs = sb("hs", [P, DBUF, NQ, T])
        yg = sb("yg", [P, DC, T])
        yt = sb("yt", [P, DC, TC, P])
        uD = sb("uD", [P, 2, T])
        x1 = sb("x1", [P, 2, TC, D])
        st1, mv1 = sb("st1", [P, TC, 6]), sb("mv1", [P, TC, 2])
        ve1, rs1, nb1 = sb("ve1", [P, TC]), sb("rs1", [P, TC]), sb("nb1", [P, TC])
        xh = sb("xh", [P, TC, D])
        xT = sb("xT", [P, KD, T])
        qmax, qsum, rq = sb("qmax", [P, TC, HEADS]), sb("qsum", [P, TC, HEADS]), sb("rq", [P, TC, HEADS])
        qe = sb("qe", [P, TC, D])
        kmax, ksum, rk = sb("kmax", [P, KD]), sb("ksum", [P, KD]), sb("rk", [P, KD])
        ke = sb("ke", [P, KD, T])
        vm = sb("vm", [P, TC, D])
        qT, kT = sb("qT", [P, KD, T]), sb("kT", [P, TC, D])
        att = sb("att", [P, KD, P])
        yq = qe
        st2, mv2 = sb("st2", [P, TC, 6]), sb("mv2", [P, TC, 2])
        ve2, rs2, nb2 = sb("ve2", [P, TC]), sb("rs2", [P, TC]), sb("nb2", [P, TC])
        fin = sb("fin", [P, TC, D])
        bc_dram = nc.dram_tensor("bc_rows", (2, 2 * N, T), F32, kind="Internal").ap()

        ring = ps("ring", [P, 2, NQ, T])
        YT = ps("YT", [P, TC, P])
        PX = ps("PX", [P, 2, T])
        PY = ps("PY", [P, 2, T])
        PZ = ps("PZ", [P, 2, T])

        split_f = BC[0:SPLIT, 1, 5 * KC:5 * KC + 4 * D // T + NB, :].rearrange("p r t -> p (r t)")
        adaT = BC[:, 1, 0:3 * KC, :].rearrange("p (k s) e -> p k s e", k=KC)
        embT = BC[:, 1, 3 * KC:5 * KC, :].rearrange("p (k s) e -> p k s e", k=KC)

        s_ld_par = sem("ld_par")
        s_ld_ident = sem("ld_ident")
        s_ld_ada = sem("ld_ada")
        s_ld_emb = sem("ld_emb")
        s_ld_win2 = sem("ld_win2")
        s_ld_win = sem("ld_win")
        s_ld_small = sem("ld_small")
        s_ld_w = sem("ld_w")
        s_ld_post = sem("ld_post")
        s_pool_const = sem("pool_const")
        s_sc_ready = sem("sc_ready")
        s_aexp_ready = sem("aexp_ready")
        s_aneg_ready = sem("aneg_ready")
        s_mod_mm = sem("mod_mm")
        s_mod_ready = sem("mod_ready")
        s_emb_mm = sem("emb_mm")
        s_emb_ready = sem("emb_ready")
        s_m0_ready = sem("m0_ready")
        s_gate8_ready = sem("gate8_ready")
        s_gate_mm = sem("gate_mm")
        s_gate_ready = sem("gate_ready")
        s_split_step = sem("split_step")
        s_split_rest = sem("split_rest")
        s_rows_ready = sem("rows_ready")
        s_st0_ready = sem("st0_ready")
        s_ve0_ready = sem("ve0_ready")
        s_rs0_ready = sem("rs0_ready")
        s_xhat_ready = sem("xhat_ready")
        s_xT_mm = sem("xT_mm")
        s_xn_ready = sem("xn_ready")
        s_xz_mm = sem("xz_mm")
        s_conv0_ready = sem("conv0_ready")
        s_tap_done = sem("tap_done")
        s_u_ready = sem("u_ready")
        s_z_ready = sem("z_ready")
        s_xp_mm = sem("xp_mm")
        s_xdbl_ready = sem("xdbl_ready")
        s_bc_stored = sem("bc_stored")
        s_dt_mm = sem("dt_mm")
        s_vpos_ready = sem("vpos_ready")
        s_vabs_ready = sem("vabs_ready")
        s_vexp_ready = sem("vexp_ready")
        s_vln_ready = sem("vln_ready")
        s_dt_sum = sem("dt_sum")
        s_dtu_ready = sem("dtu_ready")
        s_dt_ready = sem("dt_ready")
        s_da_ready = sem("da_ready")
        s_dbu_ready = sem("dbu_ready")
        s_scan_done = sem("scan_done")
        s_hc_ready = sem("hc_ready")
        s_y_acc = sem("y_acc")
        s_yt_ready = sem("yt_ready")
        s_uD_ready = sem("uD_ready")
        s_uD_added = sem("uD_added")
        s_yback_mm = sem("yback_mm")
        s_yg_ready = sem("yg_ready")
        s_out_mm = sem("out_mm")
        s_gated = sem("gated")
        s_x1_ready = sem("x1_ready")
        s_st1_ready = sem("st1_ready")
        s_ve1_ready = sem("ve1_ready")
        s_rs1_ready = sem("rs1_ready")
        s_xh_ready = sem("xh_ready")
        s_x1T_mm = sem("x1T_mm")
        s_xT_ready = sem("xT_ready")
        s_q_mm = sem("q_mm")
        s_k_mm = sem("k_mm")
        s_v_mm = sem("v_mm")
        s_qmax_ready = sem("qmax_ready")
        s_qsub_ready = sem("qsub_ready")
        s_qe_ready = sem("qe_ready")
        s_kmax_ready = sem("kmax_ready")
        s_ke_ready = sem("ke_ready")
        s_v_ready = sem("v_ready")
        s_qrec_step = sem("qrec_step")
        s_krec_ready = sem("krec_ready")
        s_qT_mm = sem("qT_mm")
        s_kT_mm = sem("kT_mm")
        s_qT_ready = sem("qT_ready")
        s_kT_ready = sem("kT_ready")
        s_nbp0 = sem("nbp0")
        s_nbp1 = sem("nbp1")
        s_nbp2 = sem("nbp2")
        s_att_mm = sem("att_mm")
        s_att_ready = sem("att_ready")
        s_y_mm = sem("y_mm")
        s_yq_ready = sem("yq_ready")
        s_st2_ready = sem("st2_ready")
        s_ve2_ready = sem("ve2_ready")
        s_rs2_ready = sem("rs2_ready")
        s_yh_ready = sem("yh_ready")
        s_yT_mm = sem("yT_mm")
        s_hT_ready = sem("hT_ready")
        s_o_mm = sem("o_mm")
        s_fin_ready = sem("fin_ready")
        x_loaded = [sem(f"x_loaded{i}") for i in range(XBUF)]
        bc_loaded = [[sem(f"bc_loaded{i}_{q}") for q in range(UPC)] for i in range(2)]
        s_out_stored = sem("out_stored")

        def pcol(name, lo=0, hi=None):
            s, e = COLS[name]
            return par[:, s + lo:(e if hi is None else s + hi)]

        def xz_bank(b, h):
            return (PX, PY, PZ, ring[:, 0, 0:2, :])[h] if b == 0 else PX

        def over_batches(col):
            return col.unsqueeze(2).to_broadcast([P, col.shape[1], NB])

        block = ctx.enter_context(nc.Block())

        @block.sync
        def _(sp):
            def load_x(b):
                if b >= XBUF:
                    sp.wait_ge(s_x1_ready, b - XBUF + 1)
                sp.dma_start(xg[:, b % XBUF], a["x"][b].rearrange("(c p) d -> p c d", p=P)).then_inc(
                    x_loaded[b % XBUF], 16)

            def broadcast_bc(b):
                if b >= 2:
                    sp.wait_ge(s_dbu_ready, U * (b - 1))
                    sp.wait_ge(s_hc_ready, U * (b - 1))
                if b == 1:
                    sp.wait_ge(s_rows_ready, 1)
                    sp.wait_ge(s_emb_mm, 2)
                sp.wait_ge(s_xdbl_ready, b + 1)
                sp.dma_start(bc_dram[b % 2], xdbl[RANK:RANK + 2 * N, :]).then_inc(s_bc_stored, 16)
                sp.wait_ge(s_bc_stored, 16 * (b + 1))
                for q in range(UPC):
                    sp.dma_start(BC[:, b % 2].rearrange("p (h n) t -> p h n t", h=2)[:, :, NQ * q:NQ * q + NQ],
                                 bc_dram[b % 2].rearrange("(h n) t -> h n t", h=2)[:, NQ * q:NQ * q + NQ].unsqueeze(
                                     0).to_broadcast([P, 2, NQ, T])).then_inc(bc_loaded[b % 2][q], 16)

            def store(b):
                sp.wait_ge(s_fin_ready, b + 1)
                sp.dma_start(out[b].rearrange("(c p) d -> p c d", p=P), fin[:, :, :]).then_inc(s_out_stored, 16)

            def load_seg(tile, src, seg, n, sem):
                sp.dma_start(tile, src[:, seg:seg + n].rearrange("(k p) e -> p k e", p=P)).then_inc(sem, 16)

            sp.dma_start(cT[:, :, :], a["cT"].rearrange("(k p) b -> p k b", p=P)).then_inc(s_ld_par, 16)
            sp.dma_start(par[:, :], a["par"]).then_inc(s_ld_par, 16)
            load_x(0)
            sp.wait_ge(s_pool_const, 3)
            for p in THIRDS:
                sp.dma_start(split_f[p:p + 1, :], a["rows"]).then_inc(s_ld_small, 16)
            load_seg(adaT[:, :, 0], a["ada_wT"], 0, D, s_ld_ada)
            load_seg(adaT[:, :, 1], a["ada_wT"], D, D, s_ld_ada)
            sp.dma_start(ident[:, :], a["ident"]).then_inc(s_ld_ident, 16)
            load_seg(win[:, :, 0:DI], a["in_wT"], 0, DI, s_ld_win)
            load_seg(win[:, :, DI:2 * DI], a["in_wT"], DI, DI, s_ld_win2)
            sp.dma_start(wxp[:, :, :], a["xp_wT"].rearrange("(k p) e -> p k e", p=P)).then_inc(s_ld_w, 16)
            sp.dma_start(wdt[0:RANK, :], a["dt_wT"]).then_inc(s_ld_w, 16)
            sp.dma_start(wdt[ONES_ROW:ONES_ROW + 1, :], a["dt_b"].unsqueeze(0)).then_inc(s_ld_w, 16)
            load_x(1)
            sp.dma_start(gb8[:, :], a["ada_b"][2 * D:3 * D].unsqueeze(0).to_broadcast([NB, D])).then_inc(s_ld_emb, 16)
            load_seg(adaT[:, :, 2], a["ada_wT"], 2 * D, D, s_ld_emb)
            load_seg(embT[:, :, 0], a["W_emb"], 0, D, s_ld_emb)
            load_seg(embT[:, :, 1], a["W_emb"], D, D, s_ld_emb)
            broadcast_bc(0)
            sp.dma_start(wo[:, :, :], a["out_wT"].rearrange("(k p) e -> p k e", p=P)).then_inc(s_ld_post, 16)
            for i, w in enumerate(("Wq", "Wk", "Wv", "W_out")):
                sp.dma_start(wqkvo[:, i], a[w].rearrange("(k p) e -> p k e", p=P)).then_inc(s_ld_post, 16)
            sp.dma_start(blockmask[:, :], a["blockmask"]).then_inc(s_ld_post, 16)
            load_x(2)
            for b in range(1, NB + 3):
                if b < NB:
                    broadcast_bc(b)
                if b >= 3:
                    store(b - 3)
                if b + 2 < NB:
                    load_x(b + 2)
            sp.wait_ge(s_out_stored, 16 * NB)

        @block.gpsimd
        def _(pool):
            nc.gpsimd.memset(split_f, 0.0).then_inc(s_pool_const, 1)
            pool.wait_ge(s_pool_const, 1)
            nc.gpsimd.memset(wdt[RANK:ONES_ROW, :], 0.0).then_inc(s_pool_const, 1)
            pool.wait_ge(s_pool_const, 2)
            nc.gpsimd.memset(xdbl[ONES_ROW:ONES_ROW + 1, :], 1.0).then_inc(s_pool_const, 1)
            pool.wait_ge(s_pool_const, 3)
            nc.gpsimd.memset(mhalf[:, :], -0.5).then_inc(s_pool_const, 1)
            pool.wait_ge(s_pool_const, 4)
            nc.gpsimd.memset(ones3[:, :], 0.0).then_inc(s_pool_const, 1)
            for i, p in enumerate(THIRDS):
                pool.wait_ge(s_pool_const, 5 + i)
                nc.gpsimd.memset(ones3[p:p + 1, :], 1.0).then_inc(s_pool_const, 1)
            pool.wait_ge(s_pool_const, 8)

            def rstd(ready, b, mv, ve, rs, nb, ve_sem, rs_sem, nbp_sem):
                pool.wait_ge(ready, 2 * TC * (b + 1))
                nc.gpsimd.tensor_scalar(ve[:, :], mv[:, :, 1], EPS, None, ALU.add).then_inc(ve_sem, 1)
                pool.wait_ge(ve_sem, b + 1)
                nc.gpsimd.tensor_tensor(rs[:, :], ve[:, :], mhalf[:, :], ALU.pow).then_inc(rs_sem, 1)
                pool.wait_ge(rs_sem, 2 * b + 1)
                nc.gpsimd.tensor_tensor(nb[:, :], mv[:, :, 0], rs[:, :], ALU.mult).then_inc(nbp_sem, 1)
                pool.wait_ge(nbp_sem, b + 1)
                nc.gpsimd.tensor_scalar(nb[:, :], nb[:, :], -1.0, None, ALU.mult).then_inc(rs_sem, 1)

            def rstd0(b):
                if b >= 1:
                    pool.wait_ge(s_xhat_ready, TC * b)
                rstd(s_st0_ready, b, mv0, ve0, rs0, nb0, s_ve0_ready, s_rs0_ready, s_nbp0)

            def softplus_sum(b, h):
                pool.wait_ge(s_vln_ready, 2 * b + h + 1)
                half = slice(2 * h, 2 * h + 2)
                nc.gpsimd.tensor_tensor(dt[:, b % 2, half], dt[:, b % 2, half], vln[:, half], ALU.add).then_inc(
                    s_dt_sum, 1)
                pool.wait_ge(s_dt_sum, 2 * b + h + 1)
                nc.gpsimd.tensor_tensor(dtu[:, b % 2, half], dt[:, b % 2, half], u[:, b % 2, half],
                                        ALU.mult).then_inc(s_dtu_ready, 1)
                pool.wait_ge(s_dtu_ready, 2 * b + h + 1)
                nc.gpsimd.memset(dt[:, b % 2, half, 0:1], BIG).then_inc(s_dt_ready, 1)

            def softplus_0(b):
                softplus_sum(b, 0)

            def softplus_1(b):
                softplus_sum(b, 1)

            def inputs_of(b, i):
                g, dc, q = U * b + i, i // UPC, i % UPC
                if dc == 0:
                    pool.wait_ge(bc_loaded[b % 2][q], 16 * (b // 2 + 1))
                if g >= DBUF:
                    pool.wait_ge(s_y_acc, g - DBUF + 1)
                nc.gpsimd.tensor_tensor(
                    hs[:, g % DBUF], dtu[:, b % 2, dc, :].unsqueeze(1).to_broadcast([P, NQ, T]),
                    BC[:, b % 2, NQ * q:NQ * q + NQ, :], ALU.mult).then_inc(s_dbu_ready, 1)

            def residual(b):
                pool.wait_ge(s_gated, b + 1)
                nc.gpsimd.tensor_tensor(x1[:, b % 2], x1[:, b % 2], xg[:, b % XBUF], ALU.add).then_inc(s_x1_ready, 1)

            def rstd1(b):
                if b >= 1:
                    pool.wait_ge(s_xh_ready, TC * b)
                rstd(s_st1_ready, b, mv1, ve1, rs1, nb1, s_ve1_ready, s_rs1_ready, s_nbp1)

            def rstd2(b):
                if b >= 1:
                    pool.wait_ge(s_yh_ready, TC * b)
                rstd(s_st2_ready, b, mv2, ve2, rs2, nb2, s_ve2_ready, s_rs2_ready, s_nbp2)

            for g in range(FIRST, LAST):
                if 0 <= g < NB * U:
                    inputs_of(g // U, g % U)
                for slot, step in ((-17, rstd0), (-3, softplus_0), (-1, softplus_1), (24, residual), (26, rstd1),
                                   (38, rstd2)):
                    b = due(g, slot)
                    if b is not None:
                        step(b)

        @block.scalar
        def _(act):
            def setup():
                act.wait_ge(s_ld_par, 32)
                nc.scalar.activation(cT[:, :, :], cT[:, :, :], ACT.Silu).then_inc(s_sc_ready, 1)
                nc.scalar.activation(Aneg[:, :], pcol("A_log"), ACT.Exp).then_inc(s_aexp_ready, 1)

            def normalize(dst, src, rs, nb, ready):
                for c in range(TC):
                    nc.scalar.activation(dst[:, c, :], src[:, c, :], ACT.Identity, bias=nb[:, c:c + 1],
                                         scale=rs[:, c:c + 1]).then_inc(ready, 1)

            def normalize0(b):
                act.wait_ge(s_rs0_ready, 2 * b + 2)
                if b >= 1:
                    act.wait_ge(s_xT_mm, b)
                normalize(xhat, xg[:, b % XBUF], rs0, nb0, s_xhat_ready)

            def modulated(b):
                act.wait_ge(s_xT_mm, b + 1)
                if b == 0:
                    act.wait_ge(s_m0_ready, 2 * KD)
                for k in range(KD):
                    nc.scalar.activation(xnT[:, k, :], PX[:, k, :], ACT.Identity, bias=m0b[:, k, b:b + 1],
                                         scale=m0s[:, k, b:b + 1]).then_inc(s_xn_ready, 1)

            def conv_last_tap(b, h):
                act.wait_ge(s_xz_mm, 4 * b + h + 1)
                if b >= 1:
                    act.wait_ge(s_dt_sum, 2 * b)
                for e in range(2):
                    dc = 2 * h + e
                    nc.scalar.activation(conv[:, dc, :], xz_bank(b, h)[:, e, :], ACT.Identity, bias=pcol("conv_b", dc, dc + 1),
                                         scale=pcol("conv_w", TAPS * dc + 3, TAPS * dc + 4)).then_inc(s_conv0_ready, 1)

            def copy_z(b):
                act.wait_ge(s_xz_mm, 4 * b + 3)
                if b >= 2:
                    act.wait_ge(s_yg_ready, 2 * (b - 1))
                nc.scalar.activation(zs[:, b % 2, 0:2, :], xz_bank(b, 2)[:, :, :], ACT.Copy).then_inc(s_z_ready, 1)

            def silu_z(b):
                act.wait_ge(s_z_ready, 3 * b + 1)
                nc.scalar.activation(zs[:, b % 2, 0:2, :], zs[:, b % 2, 0:2, :], ACT.Silu).then_inc(s_z_ready, 1)
                act.wait_ge(s_xz_mm, 4 * b + 4)
                nc.scalar.activation(zs[:, b % 2, 2:4, :], xz_bank(b, 3)[:, :, :], ACT.Silu).then_inc(s_z_ready, 1)

            def silu_u(b):
                act.wait_ge(s_tap_done, 3 * DC * (b + 1))
                if b >= 2:
                    act.wait_ge(s_uD_ready, DC * (b - 1))
                nc.scalar.activation(u[:, b % 2], conv[:, :, :], ACT.Silu).then_inc(s_u_ready, 1)

            def copy_xdbl(b):
                act.wait_ge(s_xp_mm, b + 1)
                if b >= 1:
                    act.wait_ge(s_bc_stored, 16 * b)
                nc.scalar.activation(xdbl[0:ONES_ROW, :], PX[0:ONES_ROW, 0, :], ACT.Copy).then_inc(s_xdbl_ready, 1)

            def softplus_parts(b, h):
                half = slice(2 * h, 2 * h + 2)
                act.wait_ge(s_dt_mm, 2 * b + h + 1)
                if b >= 2:
                    act.wait_ge(s_da_ready, U * (b - 1))
                    act.wait_ge(s_dtu_ready, 2 * (b - 1))
                nc.scalar.activation(dt[:, b % 2, half], PX[:, :, :], ACT.Relu).then_inc(s_vpos_ready, 1)
                act.wait_ge(s_u_ready, b + 1)
                nc.scalar.activation(vln[:, half], PX[:, :, :], ACT.Abs).then_inc(s_vabs_ready, 1)
                act.wait_ge(s_vabs_ready, 2 * b + h + 1)
                nc.scalar.activation(vln[:, half], vln[:, half], ACT.Exp, scale=-1.0).then_inc(s_vexp_ready, 1)
                act.wait_ge(s_vexp_ready, 2 * b + h + 1)
                nc.scalar.activation(vln[:, half], vln[:, half], ACT.Ln, bias=1.0).then_inc(s_vln_ready, 1)

            def skip_term(b, dc):
                if DC * b + dc >= 2:
                    act.wait_ge(s_uD_added, DC * b + dc - 1)
                nc.scalar.activation(uD[:, dc % 2, :], u[:, b % 2, dc, :], ACT.Copy,
                                     scale=pcol("D_par", dc, dc + 1)).then_inc(s_uD_ready, 1)

            def decays(b, i):
                g, dc, q = U * b + i, i // UPC, i % UPC
                if i % (U // 2) == 0:
                    act.wait_ge(s_dt_ready, 2 * b + i // (U // 2) + 1)
                if g == 0:
                    act.wait_ge(s_aneg_ready, 1)
                if g >= 2:
                    act.wait_ge(s_scan_done, g - 1)
                for j in range(NQ):
                    c = N * dc + NQ * q + j
                    ins = nc.scalar.activation(ring[:, g % 2, j, :], dt[:, b % 2, dc, :], ACT.Exp,
                                               scale=Aneg[:, c:c + 1])
                ins.then_inc(s_da_ready, 1)

            def normalize1(b):
                act.wait_ge(s_rs1_ready, 2 * b + 2)
                if b >= 1:
                    act.wait_ge(s_yT_mm, b)
                normalize(xh, x1[:, b % 2], rs1, nb1, s_xh_ready)

            def normalize2(b):
                act.wait_ge(s_rs2_ready, 2 * b + 2)
                act.wait_ge(s_x1T_mm, b + 1)
                normalize(xh, yq, rs2, nb2, s_yh_ready)

            def norm1(b):
                act.wait_ge(s_x1T_mm, b + 1)
                if b >= 1:
                    act.wait_ge(s_o_mm, b)
                for k in range(KD):
                    nc.scalar.activation(xT[:, k, :], PZ[:, k, :], ACT.Identity, bias=pcol("ln1_b", k, k + 1),
                                         scale=pcol("ln1_w", k, k + 1)).then_inc(s_xT_ready, 1)

            def exp_qk(b):
                act.wait_ge(s_qsub_ready, b + 1)
                nc.scalar.activation(qe[:, :, :], qe[:, :, :], ACT.Exp).then_inc(s_qe_ready, 1)
                act.wait_ge(s_kmax_ready, 2 * (b + 1))
                for k in range(KD):
                    nc.scalar.activation(ke[:, k, :], PZ[:, k, :], ACT.Exp, bias=kmax[:, k:k + 1],
                                         accum_out=ksum[:, k:k + 1]).then_inc(s_ke_ready, 1)

            def mask_v(b):
                act.wait_ge(s_v_mm, b + 1)
                for c in range(TC):
                    nc.scalar.activation(vm[:, c, :], PY[:, c, :], ACT.Copy,
                                         scale=pcol("mask", TC * b + c, TC * b + c + 1)).then_inc(s_v_ready, 1)

            def copy_qT(b):
                act.wait_ge(s_qT_mm, b + 1)
                nc.scalar.activation(qT[:, :, :], PZ[:, :, :], ACT.Copy).then_inc(s_qT_ready, 1)

            def copy_kT(b):
                act.wait_ge(s_kT_mm, b + 1)
                nc.scalar.activation(kT[:, :, :], PY[:, :, :], ACT.Copy).then_inc(s_kT_ready, 1)

            def silu_h(b):
                act.wait_ge(s_yT_mm, b + 1)
                act.wait_ge(s_emb_ready, 1 + 3 * KD)
                for k in range(KD):
                    nc.scalar.activation(xT[:, k, :], PZ[:, k, :], ACT.Silu, bias=m1b[:, k, b:b + 1],
                                         scale=m1s[:, k, b:b + 1]).then_inc(s_hT_ready, 1)

            def conv_last_tap_0(b):
                conv_last_tap(b, 0)

            def conv_last_tap_1(b):
                conv_last_tap(b, 1)

            def softplus_parts_0(b):
                softplus_parts(b, 0)

            def softplus_parts_1(b):
                softplus_parts(b, 1)

            def silus(b):
                if b == 0:
                    silu_u(b)
                if b < NB:
                    silu_z(b)
                if 1 <= b < NB:
                    silu_u(b)
                if b >= 3:
                    silu_h(b - 3)
                nc.scalar.preload_act_table_set("natural_log_exp_and_others")

            setup()
            for g in range(FIRST, LAST):
                if 0 <= g < NB * U:
                    decays(g // U, g % U)
                for dc in range(DC):
                    b = due(g, UPC * dc - 2)
                    if b is not None:
                        skip_term(b, dc)
                for slot, step in ((-17, normalize0), (-16, modulated), (-15, conv_last_tap_0), (-14, conv_last_tap_1),
                                   (-11, copy_z), (-6, copy_xdbl), (-5, softplus_parts_0), (-3, softplus_parts_1),
                                   (25, normalize1), (26, norm1), (30, exp_qk), (31, mask_v), (32, copy_qT),
                                   (33, copy_kT), (38, normalize2)):
                    b = due(g, slot)
                    if b is not None:
                        step(b)
                if (g + 9) % U == 0 and 0 <= (g + 9) // U < NB + 3:
                    silus((g + 9) // U)

        @block.vector
        def _(dve):
            V = nc.vector

            def stats(b, src, st, mv, ready):
                for c in range(TC):
                    V.bn_stats(st[:, c, :], src[:, c, :]).then_inc(ready, 1)
                for c in range(TC):
                    dve.wait_ge(ready, 2 * TC * b + TC)
                    V.bn_aggr(mv[:, c, :], st[:, c, :]).then_inc(ready, 1)

            def stats0(b):
                dve.wait_ge(x_loaded[b % XBUF], 16 * (b // XBUF + 1))
                if b >= 1:
                    dve.wait_ge(s_ve0_ready, b)
                stats(b, xg[:, b % XBUF], st0, mv0, s_st0_ready)

            def conv_taps(b, h):
                dve.wait_ge(s_conv0_ready, DC * b + 2 * h + 2)
                for s in range(1, TAPS):
                    for e in range(2):
                        dc = 2 * h + e
                        if s > 1:
                            dve.wait_ge(s_tap_done, 3 * DC * b + 6 * h + 2 * (s - 2) + e + 1)
                        w = pcol("conv_w", TAPS * dc + 3 - s, TAPS * dc + 4 - s)
                        V.scalar_tensor_tensor(conv[:, dc, s:], xz_bank(b, h)[:, e, 0:T - s], w, conv[:, dc, s:], ALU.mult,
                                               ALU.add).then_inc(s_tap_done, 1)

            def scan_unit(b, i):
                g = U * b + i
                q = i % UPC
                dve.wait_ge(s_da_ready, g + 1)
                dve.wait_ge(s_dbu_ready, g + 1)
                states = hs[:, g % DBUF].rearrange("p n t -> p (n t)")
                V.tensor_tensor_scan(states, ring[:, g % 2].rearrange("p n t -> p (n t)"), states, 0.0, ALU.mult,
                                     ALU.add).then_inc(s_scan_done, 1)
                dve.wait_ge(s_scan_done, g + 1)
                if i < UPC:
                    dve.wait_ge(bc_loaded[b % 2][q], 16 * (b // 2 + 1))
                V.tensor_tensor(hs[:, g % DBUF], hs[:, g % DBUF], BC[:, b % 2, N + NQ * q:N + NQ * q + NQ, :],
                                ALU.mult).then_inc(s_hc_ready, 1)

            def copy_sums(b, dc):
                dve.wait_ge(s_y_acc, U * b + UPC * (dc + 1))
                if b >= 1:
                    dve.wait_ge(s_yback_mm, 2 * b)
                V.tensor_copy(yt[:, dc], YT[:, :, :]).then_inc(s_yt_ready, 1)

            def gate_y(b):
                dve.wait_ge(s_z_ready, 3 * b + 3)
                for h, bank in ((0, PZ), (1, PY)):
                    dve.wait_ge(s_yback_mm, 2 * b + h + 1)
                    if b >= 1:
                        dve.wait_ge(s_out_mm, b)
                    V.tensor_tensor(yg[:, 2 * h:2 * h + 2, :], bank[:, :, :], zs[:, b % 2, 2 * h:2 * h + 2, :],
                                    ALU.mult).then_inc(s_yg_ready, 1)

            def gate_x(b):
                dve.wait_ge(s_out_mm, b + 1)
                if b == 0:
                    dve.wait_ge(s_gate_ready, 4)
                if b >= 2:
                    dve.wait_ge(s_fin_ready, b - 1)
                V.tensor_tensor(x1[:, b % 2], PY[:, :, :], gate[:, b, :].unsqueeze(1).to_broadcast([P, TC, D]),
                                ALU.mult).then_inc(s_gated, 1)

            def stats1(b):
                dve.wait_ge(s_x1_ready, b + 1)
                stats(b, x1[:, b % 2], st1, mv1, s_st1_ready)

            def max_qk(b):
                dve.wait_ge(s_q_mm, b + 1)
                heads = PY[:, :, :].rearrange("p c (h e) -> p (c h) e", h=HEADS)
                V.tensor_reduce(qmax[:, :, :].rearrange("p c h -> p (c h)"), heads, AX.X,
                                ALU.max).then_inc(s_qmax_ready, 1)
                dve.wait_ge(s_k_mm, b + 1)
                V.tensor_reduce(kmax[:, :], PZ[:, :, :], AX.X, ALU.max).then_inc(s_kmax_ready, 1)
                dve.wait_ge(s_qmax_ready, b + 1)
                V.tensor_tensor(qe[:, :, :].rearrange("p c (h e) -> p (c h) e", h=HEADS), heads,
                                qmax[:, :, :].rearrange("p c h -> p (c h)").unsqueeze(2).to_broadcast(
                                    [P, TC * HEADS, DH]), ALU.subtract).then_inc(s_qsub_ready, 1)
                dve.wait_ge(s_kmax_ready, 2 * b + 1)
                V.tensor_scalar(kmax[:, :], kmax[:, :], -1.0, None, ALU.mult).then_inc(s_kmax_ready, 1)

            def sums_qk(b):
                dve.wait_ge(s_qe_ready, b + 1)
                V.tensor_reduce(qsum[:, :, :].rearrange("p c h -> p (c h)"),
                                qe[:, :, :].rearrange("p c (h e) -> p (c h) e", h=HEADS), AX.X,
                                ALU.add).then_inc(s_qrec_step, 1)
                dve.wait_ge(s_ke_ready, KD * (b + 1))
                V.reciprocal(rk[:, :], ksum[:, :]).then_inc(s_krec_ready, 1)
                dve.wait_ge(s_qrec_step, 2 * b + 1)
                V.reciprocal(rq[:, :, :], qsum[:, :, :]).then_inc(s_qrec_step, 1)

            def head_blocks(b):
                dve.wait_ge(s_att_mm, b + 1)
                dve.wait_ge(s_krec_ready, b + 1)
                for k in range(KD):
                    V.scalar_tensor_tensor(att[:, k, :], PZ[:, 0, P * k:P * k + P], rk[:, k:k + 1], blockmask[:, :],
                                           ALU.mult, ALU.mult).then_inc(s_att_ready, 1)

            def normalize_q(b):
                dve.wait_ge(s_y_mm, b + 1)
                dve.wait_ge(s_qrec_step, 2 * b + 2)
                dve.wait_ge(s_qT_mm, b + 1)
                V.tensor_tensor(yq[:, :, :].rearrange("p c (h e) -> p (c h) e", h=HEADS),
                                PY[:, :, :].rearrange("p c (h e) -> p (c h) e", h=HEADS),
                                rq[:, :, :].rearrange("p c h -> p (c h)").unsqueeze(2).to_broadcast(
                                    [P, TC * HEADS, DH]), ALU.mult).then_inc(s_yq_ready, 1)

            def stats2(b):
                dve.wait_ge(s_yq_ready, b + 1)
                stats(b, yq, st2, mv2, s_st2_ready)

            def finish(b):
                dve.wait_ge(s_o_mm, b + 1)
                if b >= 1:
                    dve.wait_ge(s_out_stored, 16 * b)
                V.tensor_tensor(fin[:, :, :], PY[:, :, :], x1[:, b % 2], ALU.add).then_inc(s_fin_ready, 1)

            def setup_rows():
                count = [0]

                def step(ins):
                    count[0] += 1
                    ins.then_inc(s_split_step, 1)
                    dve.wait_ge(s_split_step, count[0])

                dve.wait_ge(s_ld_small, 3 * 16)
                dve.wait_ge(s_pool_const, 1)
                step(V.tensor_scalar(split_f[:, 4 * D:], split_f[:, 4 * D:], -1.0, MASKED, ALU.add, ALU.mult))
                step(V.tensor_copy(rows3[:, :], split_f))
                step(V.tensor_tensor(split_f, split_f, rows3[:, :], ALU.subtract))

            def setup_rows_rest():
                mid, low = THIRDS[1], THIRDS[2]
                V.tensor_copy(rows3[mid:SPLIT, :], split_f[mid:SPLIT]).then_inc(s_split_rest, 1)
                dve.wait_ge(s_split_rest, 1)
                V.tensor_tensor(split_f[low:SPLIT], split_f[low:SPLIT], rows3[low:SPLIT, :], ALU.subtract).then_inc(
                    s_split_rest, 1)
                dve.wait_ge(s_split_rest, 2)
                V.tensor_copy(rows3[low:SPLIT, :], split_f[low:SPLIT]).then_inc(s_rows_ready, 1)

            def setup():
                dve.wait_ge(s_aexp_ready, 1)
                V.tensor_scalar(Aneg[:, :], Aneg[:, :], -1.0, -1e-30, ALU.mult, ALU.min).then_inc(s_aneg_ready, 1)
                setup_rows()
                dve.wait_ge(s_mod_mm, 1)
                pm = PX[:, 0, 0:2 * KD * NB].rearrange("p (j b) -> p j b", b=NB)
                V.tensor_tensor(mods[:, 0:2 * KD, :], pm, over_batches(pcol("ada_b")), ALU.add).then_inc(s_mod_ready, 1)
                dve.wait_ge(s_mod_ready, 1)
                for k in range(KD):
                    for dst, w in ((m0s, "ln_g"), (m0b, "ln_b")):
                        V.tensor_scalar(dst[:, k, :], mods[:, KD + k, :], 1.0, pcol(w, k, k + 1), ALU.add,
                                        ALU.mult).then_inc(s_mod_ready, 1)
                dve.wait_ge(s_mod_ready, 1 + 2 * KD)
                for k in range(KD):
                    V.tensor_tensor(m0b[:, k, :], m0b[:, k, :], mods[:, k, :], ALU.add).then_inc(s_m0_ready, 2)
                setup_rows_rest()

            def setup_gate8():
                dve.wait_ge(s_emb_mm, 1)
                V.tensor_tensor(gate8[:, :], PY[0:NB, 0, :], gb8[:, :], ALU.add).then_inc(s_gate8_ready, 1)

            def add_emb_bias():
                dve.wait_ge(s_emb_mm, 2)
                pm = PZ[:, 0, 0:2 * KD * NB].rearrange("p (j b) -> p j b", b=NB)
                V.tensor_tensor(mods[:, 2 * KD:4 * KD, :], pm, over_batches(pcol("emb_b")),
                                ALU.add).then_inc(s_emb_ready, 1)
                dve.wait_ge(s_emb_ready, 1)
                for k in range(KD):
                    for dst, w in ((m1s, "ln2_w"), (m1b, "ln2_b")):
                        V.tensor_scalar(dst[:, k, :], mods[:, 2 * KD + k, :], 1.0, pcol(w, k, k + 1), ALU.add,
                                        ALU.mult).then_inc(s_emb_ready, 1)
                dve.wait_ge(s_emb_ready, 1 + 2 * KD)
                for k in range(KD):
                    V.tensor_tensor(m1b[:, k, :], m1b[:, k, :], mods[:, 3 * KD + k, :], ALU.add).then_inc(s_emb_ready, 1)

            def gate_rows(half):
                dve.wait_ge(s_gate_mm, half + 1)
                for i, bank in ((0, PY), (1, PZ)):
                    b = NB // 2 * half + 2 * i
                    V.tensor_copy(gate[:, b:b + 2, :], bank[:, :, :]).then_inc(s_gate_ready, 1)

            def gate_rows_0():
                gate_rows(0)

            def gate_rows_1():
                gate_rows(1)

            def conv_taps_0(b):
                conv_taps(b, 0)

            def conv_taps_1(b):
                conv_taps(b, 1)

            for g in range(FIRST, LAST):
                if 0 <= g < NB * U:
                    scan_unit(g // U, g % U)
                for dc in range(DC):
                    b = due(g, UPC * (dc + 1))
                    if b is not None:
                        copy_sums(b, dc)
                for slot, step in ((-23, stats0), (-16, conv_taps_0), (-14, conv_taps_1), (19, gate_y), (21, gate_x),
                                   (22, stats1), (27, max_qk), (29, sums_qk), (32, head_blocks), (33, normalize_q),
                                   (34, stats2), (40, finish)):
                    b = due(g, slot)
                    if b is not None:
                        step(b)
                if g == -21:
                    setup()
                for at, step in ((3, setup_gate8), (8, add_emb_bias), (11, gate_rows_0), (14, gate_rows_1)):
                    if g == at:
                        step()

        @block.tensor
        def _(pe):
            M = nc.tensor.matmul

            def transposes(dst, src):
                for k in range(2):
                    for c in range(2):
                        ins = nc.tensor.transpose(dst[:, k, P * c:P * c + P], src[:, c, P * k:P * k + P], ident[:, :])
                return ins

            def setup_mods(pm, w, lo):
                for j in range(2 * KD):
                    for k in range(KC):
                        ins = M(pm[:, j, :], w[:, k, lo + j // KD, P * (j % KD):P * (j % KD) + P], cT[:, k, :],
                                start=(k == 0), stop=(k == KC - 1))
                return ins

            def setup_ada():
                pe.wait_ge(s_sc_ready, 1)
                pe.wait_ge(s_ld_ada, 32)
                pm = PX[:, 0, 0:2 * KD * NB].rearrange("p (j b) -> p j b", b=NB)
                setup_mods(pm, adaT, 0).then_inc(s_mod_mm, 1)

            def setup_emb():
                pe.wait_ge(s_ld_emb, 64)
                pe.wait_ge(s_z_ready, 3)
                pe.wait_ge(s_tap_done, 3 * DC)
                for k in range(KC):
                    ins = M(PY[0:NB, 0, :], cT[:, k, :], adaT[:, k, 2], start=(k == 0), stop=(k == KC - 1))
                ins.then_inc(s_emb_mm, 1)
                pm = PZ[:, 0, 0:2 * KD * NB].rearrange("p (j b) -> p j b", b=NB)
                setup_mods(pm, embT, 0).then_inc(s_emb_mm, 1)

            def setup_gates(half):
                pe.wait_ge(s_gate8_ready, 1)
                if half == 0:
                    pe.wait_ge(s_emb_ready, 1)
                else:
                    pe.wait_ge(s_gate_ready, 2)
                for i in range(NB // 2):
                    b = NB // 2 * half + i
                    ins = M((PY, PZ)[i // 2][:, i % 2, :], ident[0:NB, b:b + 1].to_broadcast([NB, P]), gate8[:, :],
                            start=True, stop=True)
                ins.then_inc(s_gate_mm, 1)

            def setup_gates_0():
                setup_gates(0)

            def setup_gates_1():
                setup_gates(1)

            def transpose_x(b):
                pe.wait_ge(s_xhat_ready, TC * (b + 1))
                if b == 0:
                    pe.wait_ge(s_ld_ident, 16)
                    pe.wait_ge(s_mod_ready, 1)
                if b >= 1:
                    pe.wait_ge(s_vabs_ready, 2 * b)
                transposes(PX, xhat).then_inc(s_xT_mm, 1)

            def in_proj(b, h):
                if h == 0:
                    pe.wait_ge(s_xn_ready, KD * (b + 1))
                if b == 0:
                    if h == 0:
                        pe.wait_ge(s_ld_win, 16)
                    if h == 2:
                        pe.wait_ge(s_ld_win2, 16)
                elif h == 0:
                    pass
                elif h <= 2:
                    pe.wait_ge(s_tap_done, 3 * DC * b + 6 * h)
                else:
                    pe.wait_ge(s_z_ready, 3 * b + 1)
                for e in range(2):
                    lo = P * (2 * h + e)
                    for k in range(KD):
                        ins = M(xz_bank(b, h)[:, e, :], win[:, k, lo:lo + P], xnT[:, k, :], start=(k == 0), stop=(k == KD - 1))
                ins.then_inc(s_xz_mm, 1)

            def x_proj(b):
                if b >= 1:
                    pe.wait_ge(s_z_ready, 3 * b + 3)
                pe.wait_ge(s_u_ready, b + 1)
                if b == 0:
                    pe.wait_ge(s_ld_w, 48)
                    pe.wait_ge(s_pool_const, 8)
                for k in range(DC):
                    ins = M(PX[0:RANK + 2 * N, 0, :], wxp[:, k, :], u[:, b % 2, k, :], start=(k == 0),
                            stop=(k == DC - 1))
                ins.then_inc(s_xp_mm, 1)

            def dt_proj(b, h):
                if h == 0:
                    pe.wait_ge(s_xdbl_ready, b + 1)
                else:
                    pe.wait_ge(s_vabs_ready, 2 * b + 1)
                for e in range(2):
                    lo = P * (2 * h + e)
                    ins = M(PX[:, e, :], wdt[:, lo:lo + P], xdbl[:, :], start=True, stop=True)
                ins.then_inc(s_dt_mm, 1)

            def sum_states(b, i):
                g, dc, q = U * b + i, i // UPC, i % UPC
                pe.wait_ge(s_hc_ready, g + 1)
                if q == 0:
                    pe.wait_ge(s_uD_ready, DC * b + dc + 1)
                    if DC * b + dc >= 1:
                        pe.wait_ge(s_yt_ready, DC * b + dc)
                    for c in range(TC):
                        ins = M(YT[:, c, :], uD[:, dc % 2, P * c:P * c + P], ident[:, :], is_transpose=True,
                                start=(c == 0), stop=False, skip_group_check=True)
                    ins.then_inc(s_uD_added, 1)
                for j in range(NQ):
                    for c in range(TC):
                        ins = M(YT[:, c, :], hs[:, g % DBUF, j, P * c:P * c + P], ident[:, :], is_transpose=True,
                                start=False, stop=(q == UPC - 1 and j == NQ - 1 and c == TC - 1),
                                skip_group_check=True)
                ins.then_inc(s_y_acc, 1)

            def transpose_back(b):
                pe.wait_ge(s_yt_ready, DC * (b + 1))
                if b == 0:
                    pe.wait_ge(s_gate_ready, 4)
                else:
                    pe.wait_ge(s_att_ready, KD * b)
                    pe.wait_ge(s_yq_ready, b)
                for h, bank in ((0, PZ), (1, PY)):
                    for e in range(2):
                        for c in range(TC):
                            ins = nc.tensor.transpose(bank[:, e, P * c:P * c + P], yt[:, 2 * h + e, c, :], ident[:, :])
                    ins.then_inc(s_yback_mm, 1)

            def out_proj(b):
                if b == 0:
                    pe.wait_ge(s_ld_post, 16 * 6)
                    pe.wait_ge(s_rows_ready, 1)
                pe.wait_ge(s_yg_ready, 2 * (b + 1))
                for c in range(TC):
                    for k in range(DC):
                        ins = M(PY[:, c, :], yg[:, k, P * c:P * c + P], wo[:, k, :], start=(k == 0),
                                stop=(k == DC - 1))
                ins.then_inc(s_out_mm, 1)

            def transpose_x1(b):
                pe.wait_ge(s_xh_ready, TC * (b + 1))
                pe.wait_ge(s_yg_ready, 2 * b + 1)
                if b >= 1:
                    pe.wait_ge(s_hT_ready, KD * b)
                transposes(PZ, xh).then_inc(s_x1T_mm, 1)

            def rows(dst, w):
                M(dst[:, :, :], ones3[:, 0:P], rows3[:, D * w:D * w + D].unsqueeze(1).to_broadcast([SPLIT, TC, D]), start=True,
                  stop=False, skip_group_check=True)
                for c in range(TC):
                    for k in range(KD):
                        ins = M(dst[:, c, :], xT[:, k, P * c:P * c + P], wqkvo[:, w, k, :], start=False,
                                stop=(k == KD - 1), skip_group_check=True)
                return ins

            def q_and_k(b):
                pe.wait_ge(s_xT_ready, KD * (b + 1))
                pe.wait_ge(s_gated, b + 1)
                if b >= 1:
                    pe.wait_ge(s_fin_ready, b)
                rows(PY, 0).then_inc(s_q_mm, 1)
                for h in range(KD):
                    M(PZ[:, h, :], rows3[:, D + P * h:D + P * h + P], ones3[:, :], start=True, stop=False)
                    for k in range(KD):
                        M(PZ[:, h, :], wqkvo[:, 1, k, P * h:P * h + P], xT[:, k, :], start=False, stop=False)
                    ins = M(PZ[:, h, :], ones3[:, 0:P], rows3[:, 4 * D + T * b:4 * D + T * b + T], start=False, stop=True)
                ins.then_inc(s_k_mm, 1)

            def v_rows(b):
                pe.wait_ge(s_qsub_ready, b + 1)
                rows(PY, 2).then_inc(s_v_mm, 1)

            def transpose_qk(b):
                pe.wait_ge(s_qe_ready, b + 1)
                pe.wait_ge(s_ke_ready, KD * (b + 1))
                transposes(PZ, qe).then_inc(s_qT_mm, 1)
                pe.wait_ge(s_v_ready, TC * (b + 1))
                transposes(PY, ke).then_inc(s_kT_mm, 1)

            def k_times_v(b):
                pe.wait_ge(s_kT_ready, b + 1)
                pe.wait_ge(s_qT_ready, b + 1)
                for h in range(KD):
                    for c in range(TC):
                        ins = M(PZ[:, 0, P * h:P * h + P], kT[:, c, P * h:P * h + P], vm[:, c, P * h:P * h + P],
                                start=(c == 0), stop=(c == TC - 1))
                ins.then_inc(s_att_mm, 1)

            def q_times_att(b):
                pe.wait_ge(s_att_ready, KD * (b + 1))
                for c in range(TC):
                    for h in range(KD):
                        ins = M(PY[:, c, P * h:P * h + P], qT[:, h, P * c:P * c + P], att[:, h, :], start=True,
                                stop=True)
                ins.then_inc(s_y_mm, 1)

            def transpose_y(b):
                pe.wait_ge(s_yh_ready, TC * (b + 1))
                pe.wait_ge(s_yg_ready, 2 * min(b + 2, NB) - 1)
                transposes(PZ, xh).then_inc(s_yT_mm, 1)

            def output(b):
                pe.wait_ge(s_hT_ready, KD * (b + 1))
                pe.wait_ge(s_gated, min(b + 2, NB))
                rows(PY, 3).then_inc(s_o_mm, 1)

            def in_proj_0(b):
                in_proj(b, 0)

            def in_proj_1(b):
                in_proj(b, 1)

            def in_proj_2(b):
                in_proj(b, 2)

            def in_proj_3(b):
                in_proj(b, 3)

            def dt_proj_0(b):
                dt_proj(b, 0)

            def dt_proj_1(b):
                dt_proj(b, 1)

            setup_ada()
            for g in range(FIRST, LAST):
                if 0 <= g < NB * U:
                    sum_states(g // U, g % U)
                for slot, step in ((-19, transpose_x), (-18, in_proj_0), (-16, in_proj_1), (-14, in_proj_2),
                                   (-13, in_proj_3), (-9, x_proj), (-8, dt_proj_0), (-6, dt_proj_1),
                                   (18, transpose_back), (19, out_proj), (23, transpose_x1), (24, q_and_k),
                                   (28, v_rows), (29, transpose_qk), (31, k_times_v), (31, q_times_att),
                                   (35, transpose_y), (37, output)):
                    b = due(g, slot)
                    if b is not None:
                        step(b)
                for at, step in ((0, setup_emb), (8, setup_gates_0), (11, setup_gates_1)):
                    if g == at:
                        step()


def kernel(x, cond_2048, mask_BxSx1_fk1, L0_cond_ln_g, L0_cond_ln_b, L0_cond_ada_w, L0_cond_ada_b, L0_cond_in_proj_w,
           L0_cond_conv_w, L0_cond_conv_b, L0_cond_x_proj_w, L0_cond_dt_proj_w, L0_cond_dt_proj_b, L0_cond_A_log,
           L0_cond_D_param, L0_cond_out_proj_w, L1_cond_ln_w, L1_cond_ln_b, L1_cond_Wq, L1_cond_bq, L1_cond_Wk,
           L1_cond_bk, L1_cond_Wv, L1_cond_bv, L1_cond_W_emb, L1_cond_b_emb, L1_cond_ln2_w, L1_cond_ln2_b,
           L1_cond_W_out, L1_cond_b_out):
    import numpy as np
    import concourse.bacc as bacc
    from concourse.bass_utils import run_bass_kernel_spmd

    def cols(v):
        v = np.asarray(v)
        v = v.reshape(v.shape[0] // P, P, -1)
        return v.transpose(1, 0, 2).reshape(P, -1)

    par = np.concatenate([
        cols(L0_cond_A_log), cols(L0_cond_conv_w), cols(L0_cond_conv_b), cols(L0_cond_D_param),
        cols(L0_cond_ln_g), cols(L0_cond_ln_b), cols(np.asarray(L0_cond_ada_b)[:2 * D]), cols(L1_cond_b_emb),
        cols(L1_cond_ln_w), cols(L1_cond_ln_b), cols(L1_cond_ln2_w), cols(L1_cond_ln2_b),
        cols(np.asarray(mask_BxSx1_fk1).reshape(-1))], axis=1)
    heads = np.arange(P) // DH
    arrays = {
        "x": x, "cT": np.asarray(cond_2048).T, "par": par, "ident": np.eye(P, dtype=np.float32),
        "blockmask": (heads[:, None] == heads[None, :]).astype(np.float32), "ada_wT": np.asarray(L0_cond_ada_w).T,
        "ada_b": L0_cond_ada_b, "in_wT": np.asarray(L0_cond_in_proj_w).T, "xp_wT": np.asarray(L0_cond_x_proj_w).T,
        "dt_wT": np.asarray(L0_cond_dt_proj_w).T, "dt_b": L0_cond_dt_proj_b, "out_wT": np.asarray(L0_cond_out_proj_w).T, "Wq": L1_cond_Wq,
        "Wk": L1_cond_Wk, "Wv": L1_cond_Wv, "W_out": L1_cond_W_out, "W_emb": L1_cond_W_emb,
        "rows": np.concatenate([np.asarray(v).reshape(1, -1) for v in (
            L1_cond_bq, L1_cond_bk, L1_cond_bv, L1_cond_b_out, mask_BxSx1_fk1)], axis=1),
    }
    arrays = {k: np.ascontiguousarray(v) for k, v in arrays.items()}
    nc = bacc.Bacc("TRN2", target_bir_lowering=False, num_devices=1)
    aps = {k: nc.dram_tensor(f"in_{k}", v.shape, mybir.dt.from_np(v.dtype), kind="ExternalInput").ap()
           for k, v in arrays.items()}
    out = nc.dram_tensor("out", (NB, T, D), F32, kind="ExternalOutput").ap()
    build(nc, aps, out)
    r = run_bass_kernel_spmd(nc, [{f"in_{k}": v for k, v in arrays.items()}], core_ids=[0])
    return r.results[0]["out"]
```
